# Optimizing a Trainium2 kernel written in Bass

```python
import numpy as np
import jax
import jax.numpy as jnp

def _softmax(x, axis=-1):
    return jax.nn.softmax(x, axis=axis)

def _gelu(x):
    return jax.nn.gelu(x, approximate=True)

def _silu(x):
    return jax.nn.silu(x)

def _sigmoid(x):
    return jax.nn.sigmoid(x)

def _layernorm(x, axis=-1, eps=1e-05):
    m = jnp.mean(x, axis=axis, keepdims=True)
    v = jnp.var(x, axis=axis, keepdims=True)
    return (x - m) / jnp.sqrt(v + eps)

def _scatter_add(tgt, idx, src, axis=0):
    return tgt.at[idx].add(src)

def _segment_sum(src, seg, n):
    return jax.ops.segment_sum(src, seg, n)
kernel_name = 'mk_gnn_resnorm_d1_gnn_r32_53ad30'

def setup_inputs(seed: int=0):
    np.random.seed(seed)
    _w = jnp.asarray

    def _rec_inputs():
        import jax
        import jax.numpy as jnp
        _gk = jax.random.key(seed)
        x = -0.0005121 + 1.001 * jax.random.normal(jax.random.fold_in(_gk, 1), (3125, 64), jnp.float32)
        _s = jax.random.randint(jax.random.fold_in(_gk, 2), (25000,), 0, 3125, jnp.int32)
        _d = jax.random.randint(jax.random.fold_in(_gk, 3), (25000,), 0, 3125, jnp.int32)
        _loop = jnp.arange(3125, dtype=jnp.int32)
        src = jnp.concatenate([_s, _d, _loop])
        dst = jnp.concatenate([_d, _s, _loop])
        _o = jnp.argsort(dst, stable=True)
        src = src[_o]
        dst = dst[_o]
        edge_weight1 = 0.000614103 + 0.999867 * jax.random.normal(jax.random.fold_in(_gk, 12), (53125, 1), jnp.float32)
        return (x, src, dst, edge_weight1)
    x, src, dst, edge_weight1 = _rec_inputs()

    def _L0_gnn_setup():
        import jax, jax.numpy as jnp
        import numpy as np
        N_NODES = 50000
        N_EDGES = 25000
        IN_C, HID_C, OUT_C = (64, 128, 64)

        def _mp_layer(x, src, dst, edge_attr, W, b):
            n = x.shape[0]
            loops = jnp.arange(n, dtype=src.dtype)
            src2 = jnp.concatenate([src, loops])
            dst2 = jnp.concatenate([dst, loops])
            ea2 = jnp.concatenate([edge_attr, jnp.zeros((n, edge_attr.shape[1]), dtype=edge_attr.dtype)], axis=0)
            x_i = x[dst2]
            x_j = x[src2]
            msg = jnp.concatenate([x_i, x_j, ea2], axis=1) @ W + b
            agg = jax.ops.segment_sum(msg, dst2, num_segments=n)
            return jax.nn.relu(agg)
        key = jax.random.key(seed)
        k = jax.random.split(key, 8)
        x = jax.random.normal(k[0], (N_NODES, IN_C), dtype=jnp.float32)
        edge_index = jax.random.randint(k[1], (2, N_EDGES), 0, N_NODES, dtype=jnp.int64)
        edge_attr = jax.random.normal(k[2], (N_EDGES, 1), dtype=jnp.float32)
        s1 = 1.0 / np.sqrt(2 * IN_C + 1)
        s2 = 1.0 / np.sqrt(2 * HID_C + 1)
        W1 = jax.random.uniform(k[3], (2 * IN_C + 1, HID_C), jnp.float32, -s1, s1)
        b1 = jax.random.uniform(k[4], (HID_C,), jnp.float32, -s1, s1)
        W2 = jax.random.uniform(k[5], (2 * HID_C + 1, OUT_C), jnp.float32, -s2, s2)
        b2 = jax.random.uniform(k[6], (OUT_C,), jnp.float32, -s2, s2)
        return {'x': x, 'edge_index': edge_index, 'edge_attr': edge_attr, 'W1': W1, 'b1': b1, 'W2': W2, 'b2': b2}
    _L0_gnn_all = _L0_gnn_setup()
    _L0_gnn_in = {k: v for k, v in _L0_gnn_all.items() if k in ('W1', 'b1', 'W2', 'b2')}
    del _L0_gnn_all
    return {'x': x, 'src': src, 'dst': dst, 'edge_weight1': edge_weight1, 'L0_gnn_W1': _L0_gnn_in['W1'], 'L0_gnn_b1': _L0_gnn_in['b1'], 'L0_gnn_W2': _L0_gnn_in['W2'], 'L0_gnn_b2': _L0_gnn_in['b2']}

def reference(x, src, dst, edge_weight1, L0_gnn_W1, L0_gnn_b1, L0_gnn_W2, L0_gnn_b2):
    import jax
    import jax.numpy as jnp

    def _L0_gnn_ref(x, edge_index, edge_attr, W1, b1, W2, b2):
        import jax, jax.numpy as jnp
        import numpy as np
        N_NODES = 50000
        N_EDGES = 25000
        IN_C, HID_C, OUT_C = (64, 128, 64)

        def _mp_layer(x, src, dst, edge_attr, W, b):
            n = x.shape[0]
            loops = jnp.arange(n, dtype=src.dtype)
            src2 = jnp.concatenate([src, loops])
            dst2 = jnp.concatenate([dst, loops])
            ea2 = jnp.concatenate([edge_attr, jnp.zeros((n, edge_attr.shape[1]), dtype=edge_attr.dtype)], axis=0)
            x_i = x[dst2]
            x_j = x[src2]
            msg = jnp.concatenate([x_i, x_j, ea2], axis=1) @ W + b
            agg = jax.ops.segment_sum(msg, dst2, num_segments=n)
            return jax.nn.relu(agg)
        src, dst = (edge_index[0], edge_index[1])
        h = _mp_layer(x, src, dst, edge_attr, W1, b1)
        h = jax.nn.relu(h)
        out = _mp_layer(h, src, dst, edge_attr, W2, b2)
        return jax.nn.log_softmax(out, axis=1)
    edge_index = jnp.stack([src, dst])
    x = _layernorm(x + _L0_gnn_ref(x, edge_index, edge_weight1, L0_gnn_W1, L0_gnn_b1, L0_gnn_W2, L0_gnn_b2), axis=-1)
    return x

_drawn_inputs = setup_inputs


def setup_inputs(seed=0):
    import zlib

    import numpy as np

    out = dict(_drawn_inputs(seed))
    spreads = {}
    factors = {}
    for name, (base, spread) in spreads.items():
        noise = np.random.default_rng([zlib.crc32(name.encode()), seed]).standard_normal(out[name].shape)
        drawn = base * np.exp(spread * noise) if base else spread * noise
        out[name] = jnp.asarray(drawn.astype(out[name].dtype))
    for name, factor in factors.items():
        out[name] = (out[name] * factor).astype(out[name].dtype)
    return out
```

```python
import concourse.bass as bass
from concourse import mybir
from contextlib import ExitStack

FP32 = mybir.dt.float32
BF16 = mybir.dt.bfloat16
I32 = mybir.dt.int32
ALU = mybir.AluOpType
ACT = mybir.ActivationFunctionType
AX = mybir.AxisListType

N = 3125
C = 64
HID = 128
Q = 125
G = N // Q
EPS = 1e-5


def gnn(nc, x, edges, edge_attr, W1, b1, W2, b2, out, E):
    EC = E // Q
    MW = C + 2
    BANK_GROUPS = 512 // MW
    NBANK = -(-G // BANK_GROUPS)

    with ExitStack() as ctx:
        def sb(name, shape, dt):
            return ctx.enter_context(nc.sbuf_tensor(name, shape, dt))

        def pb(name, shape, dt):
            return ctx.enter_context(nc.psum_tensor(name, shape, dt))

        def sem(name):
            return ctx.enter_context(nc.semaphore(name))

        z_dram = nc.dram_tensor("z_scratch", [N, C], FP32, kind="Internal").ap()

        w1c = sb("w1c", [128, HID], FP32)
        bw1 = sb("bw1", [2, HID], FP32)
        w2c = sb("w2c", [HID, 2 * C], FP32)
        bw2 = sb("bw2", [2, C], FP32)
        ident = sb("ident", [128, 128], FP32)
        x_nat = sb("x_nat", [Q, G, C], FP32)
        base = sb("base", [Q, G, C], FP32)

        u = sb("u", [Q, 2 * C], FP32)
        v = sb("v", [Q, 2], FP32)
        ut = sb("ut", [2 * C, Q], FP32)
        vt = sb("vt", [2, Q], FP32)
        ht = sb("ht", [HID, Q], FP32)
        zs = sb("zs", [Q, 3 * C], FP32)
        t1 = sb("t1", [Q, C], FP32)
        dense = pb("dense", [128, 512], FP32)

        g_edges = sb("g_edges", [Q, EC, 2], I32)
        g_attr = sb("g_attr", [Q, EC], FP32)
        g_iota = sb("g_iota", [Q, N], FP32)
        g_onehot = sb("g_onehot", [Q, N], FP32)
        g_idx = sb("g_idx", [Q, 1], I32)
        g_msg = sb("g_msg", [Q, MW], FP32)
        g_dst = sb("g_dst", [Q, 1], FP32)
        g_free = sb("g_free", [1, 2], FP32)
        g_zero = sb("g_zero", [1, 512], FP32)
        g_sum = sb("g_sum", [Q, G, MW], FP32)
        g_acc = [pb(f"g_acc{b}", [128, 512], FP32) for b in range(NBANK)]

        f_o = sb("f_o", [Q, G, C], FP32)
        f_e = sb("f_e", [Q, G, C], FP32)
        f_m = sb("f_m", [Q, G], FP32)
        f_s = sb("f_s", [Q, G], FP32)
        f_l = sb("f_l", [Q, G], FP32)

        loaded = sem("loaded")
        x_loaded = sem("x_loaded")
        gl = sem("g_loaded")
        consts = sem("consts")
        idx_ready = sem("idx_ready")
        gathered = [sem(f"gathered{i}") for i in range(2)]
        attr_ready = [sem(f"attr_ready{i}") for i in range(2)]
        oh_ready = [sem(f"oh_ready{i}") for i in range(2)]
        chunk_done = [sem(f"chunk_done{i}") for i in range(2)]
        dve_chain = sem("dve_chain")
        acc_done = sem("acc_done")
        sum_ready = sem("sum_ready")
        u_ready = sem("u_ready")
        t_ready = sem("t_ready")
        ut_ready = sem("ut_ready")
        h_ready = sem("h_ready")
        ht_ready = sem("ht_ready")
        zp_ready = sem("zp_ready")
        zs_ready = sem("zs_ready")
        t1_ready = sem("t1_ready")
        base_ready = sem("base_ready")
        z_stored = sem("z_stored")
        fin = sem("fin")
        fin_act = sem("fin_act")
        out_stored = sem("out_stored")

        block = ctx.enter_context(nc.Block())

        @block.sync
        def _(sp):
            sp.dma_start(w1c[0:C, :], W1[C:2 * C, :]).then_inc(loaded, 16)
            sp.dma_start(w1c[C:2 * C, :], W1[0:C, :]).then_inc(loaded, 16)
            sp.dma_start(bw1[0:1, :], b1.rearrange("(a n) -> a n", a=1)).then_inc(loaded, 16)
            sp.dma_start(bw1[1:2, :], W1[2 * C:2 * C + 1, :]).then_inc(loaded, 16)
            sp.dma_start(w2c[:, 0:C], W2[HID:2 * HID, :]).then_inc(loaded, 16)
            sp.dma_start(w2c[:, C:2 * C], W2[0:HID, :]).then_inc(loaded, 16)
            sp.dma_start(bw2[0:1, :], b2.rearrange("(a n) -> a n", a=1)).then_inc(loaded, 16)
            sp.dma_start(bw2[1:2, :], W2[2 * HID:2 * HID + 1, :]).then_inc(loaded, 16)
            sp.dma_start(x_nat[:, :, :], x.rearrange("(g q) c -> q g c", q=Q)).then_inc(x_loaded, 16)
            sp.dma_start(g_edges[:, :, :], edges[0:E, :].rearrange("(p j) t -> p j t", p=Q)).then_inc(gl, 16)
            sp.dma_start(g_attr[:, :], edge_attr[0:E].rearrange("(p j) -> p j", p=Q)).then_inc(gl, 16)
            with sp.Fori(0, G) as g:
                sp.wait_ge(zs_ready, g + 1)
                sp.dma_start(z_dram[bass.ds(g * Q, Q), :], zs[:, 0:C]).then_inc(z_stored, 16)
            sp.wait_ge(fin, 13)
            sp.dma_start(out.rearrange("(g q) c -> q g c", q=Q), f_e[:, :, :]).then_inc(out_stored, 16)
            sp.wait_ge(out_stored, 16)

        @block.gpsimd
        def _(gp):
            gp.memset(g_free[:, 0:1], 0.0).then_inc(base_ready, 1)
            gp.memset(g_free[:, 1:2], 0.0).then_inc(z_stored, 16)
            gp.memset(ident[:, :], 0.0).then_inc(consts, 1)
            gp.memset(g_zero[:, :], 0.0).then_inc(consts, 1)
            gp.memset(g_msg[:, C + 1:C + 2], 1.0).then_inc(consts, 1)
            gp.iota(g_iota[:, :], [[1, N]], base=0, channel_multiplier=0,
                    allow_small_or_imprecise_dtypes=True).then_inc(consts, 1)
            gp.wait_ge(consts, 4)
            gp.affine_select(out=ident[:, :], in_=ident[:, :], compare_op=ALU.not_equal, fill=1.0,
                             base=0, pattern=[[-1, 128]], channel_multiplier=1).then_inc(consts, 1)
            gp.wait_ge(gl, 32)
            for layer, table in ((0, x), (1, z_dram)):
                if layer:
                    gp.wait_ge(z_stored, 16 * (G + 1))
                with gp.Fori(0, EC) as c:
                    gp.wait_ge(chunk_done[layer], c + 1)
                    gp.tensor_copy(g_idx[:, :], g_edges[:, bass.ds(c, 1), 0]).then_inc(idx_ready, 1)
                    gp.wait_ge(idx_ready, c + 1 + layer * EC)
                    gp.tensor_copy(g_msg[:, C:C + 1], g_attr[:, bass.ds(c, 1)]).then_inc(attr_ready[layer], 1)
                    gp.indirect_dma_start(g_msg[:, 0:C], None, table,
                                          bass.IndirectOffsetOnAxis(g_idx[:, 0:1], 0)).then_inc(gathered[layer], 16)
                if layer == 0:
                    with gp.Fori(0, G) as g:
                        gp.wait_ge(t1_ready, g + 1)
                        gp.tensor_tensor(base[:, bass.ds(g, 1), :], t1[:, :].unsqueeze(1), zs[:, 2 * C:3 * C].unsqueeze(1), ALU.add)\
                          .then_inc(base_ready, 1)

        @block.vector
        def _(dve):
            chain = [0]

            def link(ins):
                chain[0] += 1
                ins.then_inc(fin, 1)
                dve.wait_ge(fin, chain[0])

            dve.wait_ge(consts, 5)
            dve.wait_ge(gl, 32)
            for layer in range(2):
                with dve.Fori(0, EC) as c:
                    dve.wait_ge(chunk_done[layer], c + 1)
                    dve.tensor_copy(g_dst[:, :], g_edges[:, bass.ds(c, 1), 1]).then_inc(dve_chain, 1)
                    dve.wait_ge(dve_chain, c + 1 + layer * EC)
                    dve.tensor_scalar(g_onehot[:, :], g_iota[:, :], g_dst[:, 0:1], None, ALU.is_equal)\
                       .then_inc(oh_ready[layer], 1)
                dve.wait_ge(acc_done, layer + 1)
                for b in range(NBANK):
                    n = min(BANK_GROUPS, G - b * BANK_GROUPS)
                    ins = dve.tensor_copy(g_sum[:, b * BANK_GROUPS:b * BANK_GROUPS + n, :],
                                          g_acc[b][0:Q, 0:n * MW].rearrange("p (g m) -> p g m", m=MW))
                ins.then_inc(sum_ready, 1)
                dve.wait_ge(sum_ready, layer + 1)
                if layer == 0:
                    dve.wait_ge(x_loaded, 16)
                    with dve.Fori(0, G) as g:
                        dve.wait_ge(base_ready, g + 1)
                        dve.tensor_scalar(v[:, 0:1], g_sum[:, bass.ds(g, 1), C + 1], 1.0, None, ALU.add)\
                           .then_inc(u_ready, 1)
                        dve.tensor_copy(v[:, 1:2], g_sum[:, bass.ds(g, 1), C])
                        dve.tensor_tensor(u[:, 0:C].unsqueeze(1), g_sum[:, bass.ds(g, 1), 0:C],
                                          x_nat[:, bass.ds(g, 1), :], ALU.add)
                        dve.wait_ge(u_ready, 2 * g + 1)
                        dve.tensor_scalar(u[:, C:2 * C].unsqueeze(1), x_nat[:, bass.ds(g, 1), :], v[:, 0:1], None, ALU.mult)\
                           .then_inc(u_ready, 1)
                        dve.wait_ge(zs_ready, g + 1)
                        dve.scalar_tensor_tensor(out=t1[:, :], in0=dense[0:Q, C:2 * C], scalar=v[:, 0:1],
                                                 in1=zs[:, 0:C], op0=ALU.mult, op1=ALU.add).then_inc(t1_ready, 1)
            dve.wait_ge(base_ready, G + 1)
            bc = lambda t: t[:, :].unsqueeze(2).broadcast_to([Q, G, C])
            link(dve.tensor_tensor(f_o[:, :, :], g_sum[:, :, 0:C], base[:, :, :], ALU.add))
            link(dve.tensor_scalar(f_o[:, :, :], f_o[:, :, :], 0.0, None, ALU.max))
            link(dve.tensor_reduce(f_m[:, :], f_o[:, :, :], AX.X, ALU.max))
            link(dve.tensor_tensor(f_o[:, :, :], f_o[:, :, :], bc(f_m), ALU.subtract))
            dve.wait_ge(fin_act, 1)
            link(dve.tensor_reduce(f_s[:, :], f_e[:, :, :], AX.X, ALU.add))
            dve.wait_ge(fin_act, 2)
            link(dve.tensor_tensor(f_o[:, :, :], f_o[:, :, :], bc(f_l), ALU.subtract))
            link(dve.tensor_tensor(f_o[:, :, :], f_o[:, :, :], x_nat[:, :, :], ALU.add))
            link(dve.tensor_reduce(f_m[:, :], f_o[:, :, :], AX.X, ALU.add))
            link(dve.tensor_scalar(f_m[:, :], f_m[:, :], 1.0 / C, None, ALU.mult))
            link(dve.tensor_tensor(f_o[:, :, :], f_o[:, :, :], bc(f_m), ALU.subtract))
            dve.wait_ge(fin_act, 3)
            link(dve.tensor_reduce(f_s[:, :], f_e[:, :, :], AX.X, ALU.add))
            dve.wait_ge(fin_act, 4)
            link(dve.reciprocal(f_m[:, :], f_l[:, :]))
            link(dve.tensor_tensor(f_e[:, :, :], f_o[:, :, :], bc(f_m), ALU.mult))

        @block.scalar
        def _(act):
            with act.Fori(0, G) as g:
                act.wait_ge(t_ready, g + 1)
                act.activation(ut[:, :], dense[:, 0:Q], ACT.Copy)
                act.activation(vt[:, :], dense[0:2, Q:2 * Q], ACT.Copy).then_inc(ut_ready, 1)
                act.wait_ge(h_ready, g + 1)
                act.activation(ht[:, :], dense[:, 256:256 + Q], ACT.Relu).then_inc(ht_ready, 1)
                act.wait_ge(zp_ready, g + 1)
                act.wait_ge(base_ready, g + 1)
                act.wait_ge(z_stored, 16 * (g + 1))
                act.activation(zs[:, :], dense[0:Q, 0:3 * C], ACT.Copy).then_inc(zs_ready, 1)
            act.wait_ge(fin, 4)
            act.activation(f_e[:, :, :], f_o[:, :, :], ACT.Exp).then_inc(fin_act, 1)
            act.wait_ge(fin, 5)
            act.activation(f_l[:, :], f_s[:, :], ACT.Ln).then_inc(fin_act, 1)
            act.wait_ge(fin, 10)
            act.activation(f_e[:, :, :], f_o[:, :, :], ACT.Square).then_inc(fin_act, 1)
            act.wait_ge(fin, 11)
            act.activation(f_l[:, :], f_s[:, :], ACT.Sqrt, scale=1.0 / C, bias=EPS).then_inc(fin_act, 1)

        @block.tensor
        def _(pe):
            pe.wait_ge(consts, 5)
            for layer in range(2):
                if layer:
                    pe.wait_ge(sum_ready, 1)
                for b in range(NBANK):
                    ins = pe.matmul(g_acc[b][:, :], g_zero[:, 0:128], g_zero[:, :], start=True, stop=False)
                ins.then_inc(chunk_done[layer], 1)
                with pe.Fori(0, EC) as c:
                    pe.wait_ge(gathered[layer], 16 * (c + 1))
                    pe.wait_ge(attr_ready[layer], c + 1)
                    pe.wait_ge(oh_ready[layer], c + 1)
                    for g in range(G):
                        b, n = divmod(g, BANK_GROUPS)
                        ins = pe.matmul(g_acc[b][0:Q, n * MW:(n + 1) * MW], g_onehot[:, g * Q:(g + 1) * Q],
                                        g_msg[:, :], start=False, stop=False)
                    ins.then_inc(chunk_done[layer], 1)
                for b in range(NBANK):
                    ins = pe.matmul(g_acc[b][:, :], g_zero[:, 0:128], g_zero[:, :], start=False, stop=True)
                ins.then_inc(acc_done, 1)
                if layer == 0:
                    pe.wait_ge(loaded, 16 * 8)
                    with pe.Fori(0, G) as g:
                        pe.wait_ge(u_ready, 2 * g + 2)
                        pe.transpose(dense[:, 0:Q], u[:, :], ident[0:Q, 0:Q])
                        pe.transpose(dense[0:2, Q:2 * Q], v[:, :], ident[0:Q, 0:Q]).then_inc(t_ready, 1)
                        pe.wait_ge(ut_ready, g + 1)
                        pe.matmul(dense[:, 256:256 + Q], w1c[:, :], ut[:, :], start=True, stop=False)
                        pe.matmul(dense[:, 256:256 + Q], bw1[:, :], vt[:, :], start=False, stop=True).then_inc(h_ready, 1)
                        pe.wait_ge(ht_ready, g + 1)
                        pe.matmul(dense[0:Q, 0:2 * C], ht[:, :], w2c[:, :], start=True, stop=True)
                        pe.matmul(dense[0:Q, 2 * C:3 * C], vt[:, :], bw2[:, :], start=True, stop=True).then_inc(zp_ready, 1)


def kernel(x, src, dst, edge_weight1, L0_gnn_W1, L0_gnn_b1, L0_gnn_W2, L0_gnn_b2):
    import numpy as _np
    import concourse.bacc as _bacc
    from concourse import mybir as _mybir
    from concourse.bass_utils import run_bass_kernel_spmd as _run

    nc = _bacc.Bacc("TRN2", target_bir_lowering=False, num_devices=1)
    E = src.shape[0]
    arrays, args = {}, []
    edges = _np.stack([_np.asarray(src), _np.asarray(dst)], axis=1)
    edges = _np.concatenate([edges, _np.full((128, 2), N, edges.dtype)], axis=0)
    attr = _np.concatenate([_np.asarray(edge_weight1)[:, 0], _np.zeros(128, _np.float32)])
    for name, a in (("x", x), ("edges", edges), ("edge_attr", attr), ("W1", L0_gnn_W1), ("b1", L0_gnn_b1),
                    ("W2", L0_gnn_W2), ("b2", L0_gnn_b2)):
        a = _np.ascontiguousarray(a)
        arrays[f"in_{name}"] = a
        args.append(nc.dram_tensor(f"in_{name}", a.shape, _mybir.dt.from_np(a.dtype), kind="ExternalInput").ap())
    out = nc.dram_tensor("out_0", [N, C], _mybir.dt.float32, kind="ExternalOutput").ap()
    gnn(nc, *args, out, E)
    r = _run(nc, [arrays], core_ids=[0])
    return r.results[0]["out_0"]
```

```python
import concourse.bass as bass
from concourse import mybir
from contextlib import ExitStack

FP32 = mybir.dt.float32
BF16 = mybir.dt.bfloat16
I32 = mybir.dt.int32
ALU = mybir.AluOpType
ACT = mybir.ActivationFunctionType
AX = mybir.AxisListType

N = 3125
C = 64
HID = 128
Q = 125
G = N // Q
EPS = 1e-5

SLOTS = 128
WD = 5
K = N // WD
KG = Q // WD
J = K // Q
LO = N // G
PW = 3 * C
SETS = ((0, 8, 0), (9, 8, 10), (17, 8, 18))
SINGLE = 8
KW = 26
ROUND = 12582912.0
BATCHES = ((0, 6), (6, 12), (12, 18), (18, 23), (23, 25))



def gnn(nc, x, dst, edges, edge_attr, W1, b1, W2, b2, out, E):
    EC = E // Q
    BG = max(b - a for a, b in BATCHES)

    with ExitStack() as ctx:
        def sb(name, shape, dt):
            return ctx.enter_context(nc.sbuf_tensor(name, shape, dt))

        def pb(name, shape, dt):
            return ctx.enter_context(nc.psum_tensor(name, shape, dt))

        def sem(name):
            return ctx.enter_context(nc.semaphore(name))

        z3_dram = nc.dram_tensor("z3_scratch", [N, PW], BF16, kind="Internal").ap()
        se_dram = nc.dram_tensor("se_scratch", [N], FP32, kind="Internal").ap()

        w1c = sb("w1c", [128, HID], FP32)
        bw1 = sb("bw1", [2, HID], FP32)
        w2c = sb("w2c", [HID, 2 * C], FP32)
        bw2 = sb("bw2", [2, C], FP32)
        ident = sb("ident", [128, 128], FP32)
        iota2 = sb("iota2", [128, SLOTS, 2], BF16)
        thr = sb("thr", [Q, J], FP32)
        ones = sb("ones", [Q, EC], BF16)
        x_nat = sb("x_nat", [Q, G, C], FP32)
        base = sb("base", [Q, G, C], FP32)
        stats = sb("stats", [Q, G, 2], FP32)

        adj = sb("adj", [128, G * G * Q + 1], BF16)
        adj4 = adj[:, 0:G * G * Q].rearrange("p (g h e) -> p g h e", g=G, h=G)
        free = [G * G * Q]

        def tail(shape, dt):
            n = 1
            for s in shape[1:]:
                n *= s
            n *= 2 if dt in (FP32, I32) else 1
            free[0] -= n + n % 2
            ap = adj[0:shape[0], free[0] - free[0] % 2:free[0] - free[0] % 2 + n]
            free[0] -= free[0] % 2
            if dt is not BF16:
                ap = ap.bitcast(dt)
            if len(shape) == 3:
                ap = ap.rearrange("p (a b) -> p a b", a=shape[1])
            return ap

        x_lo = tail([LO, G, C], FP32)
        x_rest = tail([LO, G, C], FP32)
        x_rest2 = tail([LO, G, C], FP32)
        samp = tail([Q, 1], I32)
        samp_b = tail([Q, Q], FP32)
        junk = tail([Q, EC], BF16)
        cnt1 = tail([Q, J], FP32)
        cnt2 = tail([Q, J], FP32)
        row_idx = tail([Q, J], I32)
        off_idx = tail([Q, J], I32)
        rows = tail([Q, J, EC], I32)
        pairs = tail([Q, J, 2 * SLOTS], I32)
        attrs = tail([Q, J, SLOTS], FP32)
        lo_q = tail([Q, J, SLOTS], FP32)
        lo_f = tail([Q, J, SLOTS], FP32)
        hi_f = tail([Q, J, SLOTS], FP32)
        d_f = tail([Q, J, SLOTS], FP32)
        w_f = tail([Q, J, SLOTS], FP32)
        p_f = tail([Q, J, SLOTS], FP32)
        m_f = tail([Q, J, SLOTS], FP32)
        key_f = tail([Q, J, SLOTS], FP32)
        se_w = tail([Q, J, WD], FP32)
        se_junk = tail([Q, J * WD, SLOTS], BF16)
        assert free[0] >= 13 * G * Q

        keyl = sb("keyl", [128, G, KW], BF16)
        keyr = sb("keyr", [128, G, KW], BF16)
        ohl = [sb(f"ohl{s}", [128, 5 if s == 0 else 4, SLOTS, 2], BF16) for s in range(3)]
        ohr = [sb(f"ohr{s}", [128, 5 if s == 0 else 4, G * WD, 2], BF16) for s in range(3)]
        parts = sb("parts", [LO, G * (PW + 1)], BF16)
        x3 = parts[:, :].rearrange("p (h c) -> p h c", h=G)
        z3 = parts[:, 0:G * PW].rearrange("p (h c) -> p h c", h=G)

        s_sum = sb("s_sum", [Q, C], FP32)
        u = sb("u", [Q, 2 * C], FP32)
        ut = sb("ut", [2 * C, Q], FP32)
        vt = sb("vt", [2, Q], FP32)
        ht = sb("ht", [HID, Q], FP32)
        zs = sb("zs", [Q, 3 * C], FP32)
        zr = sb("zr", [Q, C], FP32)
        zp = sb("zp", [Q, PW], BF16)
        t1 = sb("t1", [Q, C], FP32)
        t2 = sb("t2", [Q, C], FP32)

        f_o = sb("f_o", [Q, BG, C], FP32)
        f_p = sb("f_p", [Q, BG, C], FP32)
        f_e = sb("f_e", [Q, BG, C], FP32)
        f_v = sb("f_v", [Q, 2, BG, C], FP32)
        f_m = sb("f_m", [Q, BG], FP32)
        f_s = sb("f_s", [Q, BG], FP32)
        f_l = sb("f_l", [Q, BG], FP32)
        f_bn = sb("f_bn", [Q, BG, 6], FP32)
        f_mv = sb("f_mv", [Q, BG, 2], FP32)
        f_r = sb("f_r", [Q, BG], FP32)

        pset = [pb(f"pset{s}", [128, 2, 512], FP32) for s in range(3)]
        acc = pb("acc", [128, 512], FP32)
        dense = pb("dense", [128, 512], FP32)

        def bank2(g):
            return pset[(g // 2) % 3][:, g % 2, 0:PW]


        MW = C + 2
        BANK_GROUPS = 512 // MW
        NBANK = -(-G // BANK_GROUPS)
        gz_dram = nc.dram_tensor("gz_scratch", [N, C], FP32, kind="Internal").ap()
        deg_sum = sb("deg_sum", [Q, 1], FP32)
        ones_f = sb("ones_f", [Q, 1], FP32)
        flag = sb("flag", [1, 1], I32)
        free[0] = G * G * Q
        g_edges = tail([Q, EC, 2], I32)
        g_attr = tail([Q, EC], FP32)
        g_iota = tail([Q, N], FP32)
        g_onehot = tail([Q, N], FP32)
        g_idx = tail([Q, 1], I32)
        g_msg = tail([Q, MW], FP32)
        g_dst = tail([Q, 1], FP32)
        g_free = tail([1, 2], FP32)
        g_zero = tail([1, 512], FP32)
        g_sum = tail([Q, G, MW], FP32)
        g_v = tail([Q, 2], FP32)
        go = tail([Q, G, C], FP32)
        ge = tail([Q, G, C], FP32)
        gm = tail([Q, G], FP32)
        gs = tail([Q, G], FP32)
        gw = tail([Q, G], FP32)
        g_acc = [pset[b // 2][:, b % 2, :] for b in range(NBANK)]
        assert free[0] >= 0
        deg_ready = sem("deg_ready")
        degs_ready = sem("degs_ready")
        flag_ready = sem("flag_ready")
        g_sems = {n: sem("g_" + n) for n in (
            "loaded", "consts", "idx_ready", "attr_ready0", "attr_ready1", "gathered0", "gathered1",
            "oh_ready0", "oh_ready1", "chunk_done0", "chunk_done1", "dst_ready", "acc_done", "sum_ready",
            "u_ready", "t_ready", "ut_ready", "h_ready", "ht_ready", "zp_ready", "zs_ready", "t1_ready",
            "base_ready", "z_stored", "fin", "fin_act", "out_stored")}

        samp_in = sem("samp_in")
        xlo_in = sem("xlo_in")
        w_in = sem("w_in")
        xnat_in = sem("xnat_in")
        rows_in = [sem(f"rows_in{j}") for j in range(J)]
        pairs_in = [sem(f"pairs_in{j}") for j in range(J)]
        attrs_in = [sem(f"attrs_in{j}") for j in range(J)]
        se_out = sem("se_out")
        se_in = sem("se_in")
        z_out = sem("z_out")
        z_in = sem("z_in")
        o_out = [sem("o_out0"), sem("o_out1")]
        consts = sem("consts")
        sampb_ready = sem("sampb_ready")
        sampm_ready = sem("sampm_ready")
        rowidx_ready = sem("rowidx_ready")
        off_ready = sem("off_ready")
        key_ready = sem("key_ready")
        keyt_done = sem("keyt_done")
        keys_ready = sem("keys_ready")
        xs_act = sem("xs_act")
        xs_dve = sem("xs_dve")
        se_ready = sem("se_ready")
        dch = sem("dve_chain")
        oh_ready = [sem(f"oh_ready{s}") for s in range(3)]
        built = [sem(f"built{s}") for s in range(4)]
        evac = [sem(f"evac{s}") for s in range(4)]
        acc_done = sem("acc_done")
        acc_read = sem("acc_read")
        u_ready = sem("u_ready")
        t_ready = sem("t_ready")
        ut_ready = sem("ut_ready")
        h_ready = sem("h_ready")
        ht_ready = sem("ht_ready")
        zp_ready = sem("zp_ready")
        zs_ready = sem("zs_ready")
        z3_ready = sem("z3_ready")
        base_ready = sem("base_ready")
        pch = sem("pool_chain")
        acc2_done = sem("acc2_done")
        acc2_read = sem("acc2_read")
        fch = sem("final_chain")
        fact = sem("final_act")

        block = ctx.enter_context(nc.Block())

        @block.sync
        def _(sp):
            with nc.allow_non_contiguous_dma(reason="one target per partition"):
                sp.dma_start(samp, dst[:, 0:1]).then_inc(samp_in, 16)
            sp.dma_start(x_lo, x.rearrange("(p h) c -> p h c", p=LO)).then_inc(xlo_in, 16)
            sp.dma_start(w1c[0:C, :], W1[C:2 * C, :]).then_inc(w_in, 16)
            sp.dma_start(w1c[C:2 * C, :], W1[0:C, :]).then_inc(w_in, 16)
            sp.dma_start(bw1[0:1, :], b1.rearrange("(a n) -> a n", a=1)).then_inc(w_in, 16)
            sp.dma_start(bw1[1:2, :], W1[2 * C:2 * C + 1, :]).then_inc(w_in, 16)
            sp.dma_start(w2c[:, 0:C], W2[HID:2 * HID, :]).then_inc(w_in, 16)
            sp.dma_start(w2c[:, C:2 * C], W2[0:HID, :]).then_inc(w_in, 16)
            sp.dma_start(bw2[0:1, :], b2.rearrange("(a n) -> a n", a=1)).then_inc(w_in, 16)
            sp.dma_start(bw2[1:2, :], W2[2 * HID:2 * HID + 1, :]).then_inc(w_in, 16)
            sp.dma_start(x_nat[:, :, :], x.rearrange("(g q) c -> q g c", q=Q)).then_inc(xnat_in, 16)
            sp.wait_ge(se_ready, J * WD)
            with nc.allow_non_contiguous_dma(reason="one number per node"):
                sp.dma_start(se_dram.rearrange("(j p r) -> p j r", p=Q, r=WD), se_w).then_inc(se_out, 16)
                sp.wait_ge(se_out, 16)
                sp.dma_start(stats[:, :, 1], se_dram.rearrange("(g q) -> q g", q=Q)).then_inc(se_in, 16)
            for h in range(G):
                sp.wait_ge(z3_ready, h + 1)
                sp.dma_start(z3_dram[h * Q:(h + 1) * Q, :], zp[:, :]).then_inc(z_out, 16)
            sp.wait_ge(z_out, 16 * G)
            sp.wait_ge(acc_done, G)
            sp.dma_start(z3, z3_dram.rearrange("(p h) c -> p h c", p=LO)).then_inc(z_in, 16)
            for i, (a, b) in enumerate(BATCHES):
                sp.wait_ge(fch, 11 * (i + 1))
                sp.dma_start(out[a * Q:b * Q, :].rearrange("(g q) c -> q g c", q=Q),
                             f_v[:, i % 2, 0:b - a, :]).then_inc(o_out[i % 2], 16)

            sp.wait_ge(flag_ready, 1)
            sp.wait_ge(o_out[0], 16 * ((len(BATCHES) + 1) // 2))
            sp.wait_ge(o_out[1], 16 * (len(BATCHES) // 2))
            missed = sp.value_load(flag[0:1, 0:1], min_val=0, max_val=1)
            with sp.If(missed):
                sp.dma_start(g_edges[:, :, :], edges[0:E, :].rearrange("(p j) t -> p j t", p=Q)).then_inc(g_sems["loaded"], 16)
                sp.dma_start(g_attr[:, :], edge_attr[0:E, 0].rearrange("(p j) -> p j", p=Q)).then_inc(g_sems["loaded"], 16)
                with sp.Fori(0, G) as g:
                    sp.wait_ge(g_sems["zs_ready"], g + 1)
                    sp.dma_start(gz_dram[bass.ds(g * Q, Q), :], zs[:, 0:C]).then_inc(g_sems["z_stored"], 16)
                sp.wait_ge(g_sems["fin"], 13)
                sp.dma_start(out.rearrange("(g q) c -> q g c", q=Q), ge[:, :, :]).then_inc(g_sems["out_stored"], 16)
                sp.wait_ge(g_sems["out_stored"], 16)

        @block.gpsimd
        def _(gp):
            gp.memset(ident[:, :], 0.0).then_inc(consts, 1)
            gp.iota(thr[:, :], [[Q * WD, J]], base=0, channel_multiplier=WD,
                    allow_small_or_imprecise_dtypes=True).then_inc(consts, 1)
            gp.wait_ge(consts, 2)
            gp.affine_select(out=ident[:, :], in_=ident[:, :], compare_op=ALU.not_equal, fill=1.0,
                             base=0, pattern=[[-1, 128]], channel_multiplier=1).then_inc(consts, 1)
            gp.memset(ones[:, :], 1.0).then_inc(consts, 1)
            gp.memset(ones_f[:, :], 1.0)
            gp.iota(iota2[:, :, :], [[1, SLOTS], [0, 2]], base=0, channel_multiplier=0,
                    allow_small_or_imprecise_dtypes=True).then_inc(consts, 1)
            gp.memset(keyl[:, :, SINGLE + 1:SINGLE + 2], 0.0).then_inc(consts, 1)
            gp.memset(keyr[:, :, SINGLE + 1:SINGLE + 2], 0.0).then_inc(consts, 1)
            gp.memset(x3[:, :, PW:PW + 1], 1.0).then_inc(consts, 1)
            gp.wait_ge(rowidx_ready, 1)
            for j in range(J):
                gp.indirect_dma_start(rows[:, j, :], None, dst,
                                      bass.IndirectOffsetOnAxis(row_idx[:, j:j + 1], 0)).then_inc(rows_in[j], 16)
            for j in range(J):
                gp.wait_ge(off_ready, j + 1)
                gp.indirect_dma_start(pairs[:, j, :], None, edges,
                                      bass.IndirectOffsetOnAxis(off_idx[:, j:j + 1], 0)).then_inc(pairs_in[j], 16)
            for j in range(J):
                gp.indirect_dma_start(attrs[:, j, :], None, edge_attr,
                                      bass.IndirectOffsetOnAxis(off_idx[:, j:j + 1], 0)).then_inc(attrs_in[j], 16)
            gp.wait_ge(xnat_in, 16)
            gp.wait_ge(se_in, 16)
            n = 0
            for h in range(G):
                deg = stats[:, h, 0:1]
                gp.wait_ge(acc_read, h + 1)
                if h >= 1:
                    gp.wait_ge(t_ready, h)
                gp.tensor_tensor(u[:, 0:C], s_sum[:, :], x_nat[:, h, :], ALU.add)
                gp.tensor_scalar(u[:, C:2 * C], x_nat[:, h, :], deg, None, ALU.mult).then_inc(u_ready, 1)
                gp.wait_ge(zs_ready, h + 1)
                if h >= 1:
                    gp.wait_ge(z_out, 16 * h)
                gp.tensor_copy(zp[:, 0:C], zs[:, 0:C]).then_inc(pch, 1)
                gp.tensor_scalar(t1[:, :], zs[:, C:2 * C], deg, None, ALU.mult).then_inc(pch, 1)
                gp.wait_ge(pch, n + 1)
                gp.tensor_tensor(zr[:, :], zs[:, 0:C], zp[:, 0:C], ALU.subtract).then_inc(pch, 1)
                gp.wait_ge(pch, n + 2)
                gp.tensor_tensor(t2[:, :], t1[:, :], zs[:, 0:C], ALU.add).then_inc(pch, 1)
                gp.wait_ge(pch, n + 3)
                gp.tensor_copy(zp[:, C:2 * C], zr[:, :]).then_inc(pch, 1)
                gp.wait_ge(pch, n + 4)
                gp.tensor_tensor(base[:, h, :], t2[:, :], zs[:, 2 * C:3 * C], ALU.add).then_inc(base_ready, 1)
                gp.wait_ge(pch, n + 5)
                gp.tensor_tensor(zp[:, 2 * C:3 * C], zr[:, :], zp[:, C:2 * C], ALU.subtract).then_inc(z3_ready, 1)
                n += 5

            gp.wait_ge(flag_ready, 1)
            gp.wait_ge(o_out[0], 16 * ((len(BATCHES) + 1) // 2))
            gp.wait_ge(o_out[1], 16 * (len(BATCHES) // 2))
            missed = gp.value_load(flag[0:1, 0:1], min_val=0, max_val=1)
            with gp.If(missed):
                gp.memset(g_free[:, 0:1], 0.0).then_inc(g_sems["base_ready"], 1)
                gp.memset(g_free[:, 1:2], 0.0).then_inc(g_sems["z_stored"], 16)
                gp.memset(g_zero[:, :], 0.0).then_inc(g_sems["consts"], 1)
                gp.memset(g_msg[:, C + 1:C + 2], 1.0).then_inc(g_sems["consts"], 1)
                gp.iota(g_iota[:, :], [[1, N]], base=0, channel_multiplier=0,
                        allow_small_or_imprecise_dtypes=True).then_inc(g_sems["consts"], 1)
                gp.wait_ge(g_sems["loaded"], 32)
                for layer, table in ((0, x), (1, gz_dram)):
                    if layer:
                        gp.wait_ge(g_sems["z_stored"], 16 * (G + 1))
                    with gp.Fori(0, EC) as c:
                        gp.wait_ge(g_sems[f"chunk_done{layer}"], c + 1)
                        gp.tensor_copy(g_idx[:, :], g_edges[:, bass.ds(c, 1), 0]).then_inc(g_sems["idx_ready"], 1)
                        gp.wait_ge(g_sems["idx_ready"], c + 1 + layer * EC)
                        gp.tensor_copy(g_msg[:, C:C + 1], g_attr[:, bass.ds(c, 1)]).then_inc(g_sems[f"attr_ready{layer}"], 1)
                        gp.indirect_dma_start(g_msg[:, 0:C], None, table,
                                              bass.IndirectOffsetOnAxis(g_idx[:, 0:1], 0)).then_inc(g_sems[f"gathered{layer}"], 16)
                    if layer == 0:
                        with gp.Fori(0, G) as g:
                            gp.wait_ge(g_sems["t1_ready"], g + 1)
                            gp.tensor_tensor(base[:, bass.ds(g, 1), :], t1[:, :].unsqueeze(1), zs[:, 2 * C:3 * C].unsqueeze(1), ALU.add)\
                              .then_inc(g_sems["base_ready"], 1)

        @block.vector
        def _(dve):
            chain = [0]

            def link(ins):
                chain[0] += 1
                ins.then_inc(dch, 1)
                dve.wait_ge(dch, chain[0])

            dve.wait_ge(samp_in, 16)
            dve.tensor_copy(samp_b, samp.broadcast_to([Q, Q])).then_inc(sampb_ready, 1)
            dve.wait_ge(sampm_ready, 1)
            dve.wait_ge(consts, 4)
            for j in range(J):
                ins = dve.scalar_tensor_tensor(out=junk[:, 0:Q], in0=acc[0:Q, 0:Q], scalar=thr[:, j:j + 1],
                                               in1=ones[:, 0:Q], op0=ALU.is_lt, op1=ALU.mult,
                                               accum_out=cnt1[:, j:j + 1])
                link(ins)
            dve.tensor_scalar(row_idx, cnt1, -1.0, 0.0, ALU.add, ALU.max).then_inc(rowidx_ready, 1)
            dve.wait_ge(xs_act, 1)
            dve.tensor_tensor(x_rest, x_lo, x3[:, :, 0:C], ALU.subtract).then_inc(xs_dve, 1)
            for j in range(J):
                dve.wait_ge(rows_in[j], 16)
                link(dve.scalar_tensor_tensor(out=junk[:, :], in0=rows[:, j, :], scalar=thr[:, j:j + 1],
                                              in1=ones[:, :], op0=ALU.is_lt, op1=ALU.mult,
                                              accum_out=cnt2[:, j:j + 1]))
                dve.scalar_tensor_tensor(out=off_idx[:, j:j + 1], in0=row_idx[:, j:j + 1], scalar=float(EC),
                                         in1=cnt2[:, j:j + 1], op0=ALU.mult, op1=ALU.add).then_inc(off_ready, 1)
            dve.wait_ge(xs_act, 2)
            dve.tensor_tensor(x3[:, :, 2 * C:PW], x_rest, x3[:, :, C:2 * C], ALU.subtract).then_inc(xs_dve, 1)
            for j in range(J):
                dve.wait_ge(pairs_in[j], 16)
                pv = pairs[:, j, :].rearrange("p (s t) -> p s t", t=2)
                srcs, dsts = pv[:, :, 0], pv[:, :, 1]
                dve.tensor_scalar(d_f[:, j, :], dsts, thr[:, j:j + 1], None, ALU.subtract)
                link(dve.tensor_scalar(lo_q[:, j, :], srcs, 1.0 / G, 0.5 / G - 0.5, ALU.mult, ALU.add))
                link(dve.tensor_scalar(lo_f[:, j, :], lo_q[:, j, :], ROUND, ROUND, ALU.add, ALU.subtract))
                dve.scalar_tensor_tensor(out=w_f[:, j, :], in0=d_f[:, j, :], scalar=-float(WD - 1), in1=d_f[:, j, :],
                                         op0=ALU.add, op1=ALU.mult)
                link(dve.scalar_tensor_tensor(out=hi_f[:, j, :], in0=lo_f[:, j, :], scalar=-float(G), in1=srcs,
                                              op0=ALU.mult, op1=ALU.add))
                dve.tensor_scalar(p_f[:, j, :], w_f[:, j, :], 0.0, 8192.0, ALU.is_gt, ALU.mult)
                link(dve.scalar_tensor_tensor(out=m_f[:, j, :], in0=hi_f[:, j, :], scalar=float(WD), in1=d_f[:, j, :],
                                              op0=ALU.mult, op1=ALU.add))
                dve.tensor_tensor(key_f[:, j, :], m_f[:, j, :], p_f[:, j, :], ALU.add).then_inc(key_ready, 1)

            def onehots(g, s):
                w0, n, k0 = SETS[s]
                n = (n + 1) // 2 + (s == 0)
                if g >= 1:
                    dve.wait_ge(built[s], g)
                    if s == 0:
                        dve.wait_ge(built[3], g)
                for oh, key, width in ((ohl, keyl, SLOTS), (ohr, keyr, G * WD)):
                    ins = dve.tensor_tensor(
                        out=oh[s][:, :, :, :],
                        in0=iota2[:, 0:width, :].unsqueeze(1).broadcast_to([128, n, width, 2]),
                        in1=key[:, g, k0:k0 + 2 * n].rearrange("p (q o k) -> p q o k", o=1, k=2)
                        .broadcast_to([128, n, width, 2]),
                        op=ALU.is_equal)
                ins.then_inc(oh_ready[s], 1)

            for g in range(2):
                if g == 0:
                    dve.wait_ge(keys_ready, 1)
                    dve.wait_ge(consts, 8)
                for s in range(3):
                    onehots(g, s)
            for j in range(J):
                dve.wait_ge(attrs_in[j], 16)
                for r in range(WD):
                    dve.scalar_tensor_tensor(out=se_junk[:, j * WD + r, :], in0=d_f[:, j, :], scalar=float(r),
                                             in1=attrs[:, j, :], op0=ALU.is_equal, op1=ALU.mult,
                                             accum_out=se_w[:, j, r:r + 1]).then_inc(se_ready, 1)

            for h in range(G):
                dve.wait_ge(acc_done, h + 1)
                if h >= 1:
                    dve.wait_ge(u_ready, h)
                dve.tensor_reduce(s_sum[:, :], acc[0:Q, 0:PW].rearrange("p (t c) -> p c t", t=3), AX.X, ALU.add)
                dve.tensor_scalar(stats[:, h, 0:1], acc[0:Q, PW:PW + 1], 1.0, None, ALU.add).then_inc(acc_read, 1)
                if h + 2 < G:
                    if (h + 2) % 5 == 0:
                        dve.wait_ge(keys_ready, (h + 2) // 5 + 1)
                    for s in range(3):
                        onehots(h + 2, s)

            dve.wait_ge(acc_read, G)
            dve.tensor_reduce(deg_sum[:, :], stats[:, :, 0], AX.X, ALU.add).then_inc(deg_ready, 1)

            fc = [0]

            def flink(ins):
                fc[0] += 1
                ins.then_inc(fch, 1)
                dve.wait_ge(fch, fc[0])

            na = 0
            for i, (a, b) in enumerate(BATCHES):
                n = b - a
                o, p, e, vv = f_o[:, 0:n, :], f_p[:, 0:n, :], f_e[:, 0:n, :], f_v[:, i % 2, 0:n, :]

                def bc(t):
                    return t[:, 0:n].unsqueeze(2).broadcast_to([Q, n, C])

                for g in range(a, b):
                    dve.wait_ge(acc2_done, g + 1)
                    dve.tensor_reduce(f_o[:, g - a, :], bank2(g)[0:Q, :].rearrange("p (t c) -> p c t", t=3),
                                      AX.X, ALU.add).then_inc(acc2_read, 1)
                dve.wait_ge(acc2_read, b)
                if i == 0:
                    dve.wait_ge(base_ready, G)
                flink(dve.tensor_tensor(p, o, base[:, a:b, :], ALU.add))
                flink(dve.tensor_scalar(p, p, 0.0, None, ALU.max))
                flink(dve.tensor_reduce(f_m[:, 0:n], p, AX.X, ALU.max))
                flink(dve.tensor_tensor(o, p, bc(f_m), ALU.subtract))
                dve.wait_ge(fact, na + 1)
                flink(dve.tensor_reduce(f_s[:, 0:n], e, AX.X, ALU.add))
                flink(dve.tensor_tensor(p, o, x_nat[:, a:b, :], ALU.add))
                dve.wait_ge(fact, na + 2)
                if i >= 2:
                    dve.wait_ge(o_out[i % 2], 16 * (i // 2))
                flink(dve.tensor_tensor(o, p, bc(f_l), ALU.subtract))
                for k in range(n):
                    ins = dve.bn_stats(f_bn[:, k, :], o[:, k, :])
                flink(ins)
                for k in range(n):
                    ins = dve.bn_aggr(f_mv[:, k, :], f_bn[:, k, :])
                flink(ins)
                dve.wait_ge(fact, na + 3)
                flink(dve.reciprocal(f_r[:, 0:n], f_s[:, 0:n]))
                for k in range(n):
                    ins = dve.tensor_scalar(vv[:, k, :], o[:, k, :], f_mv[:, k, 0:1], f_r[:, k:k + 1],
                                            ALU.subtract, ALU.mult)
                flink(ins)
                na += 3
                if i == 1:
                    dve.wait_ge(degs_ready, 1)
                    dve.tensor_scalar(flag[:, :], dense[0:1, 0:1], float(E + N), None, ALU.not_equal)\
                       .then_inc(flag_ready, 1)

            dve.wait_ge(flag_ready, 1)
            dve.wait_ge(o_out[0], 16 * ((len(BATCHES) + 1) // 2))
            dve.wait_ge(o_out[1], 16 * (len(BATCHES) // 2))
            missed = dve.value_load(flag[0:1, 0:1], min_val=0, max_val=1)
            with dve.If(missed):
                chain = [0]

                def link(ins):
                    chain[0] += 1
                    ins.then_inc(g_sems["fin"], 1)
                    dve.wait_ge(g_sems["fin"], chain[0])

                dve.wait_ge(g_sems["consts"], 3)
                dve.wait_ge(g_sems["loaded"], 32)
                for layer in range(2):
                    with dve.Fori(0, EC) as c:
                        dve.wait_ge(g_sems[f"chunk_done{layer}"], c + 1)
                        dve.tensor_copy(g_dst[:, :], g_edges[:, bass.ds(c, 1), 1]).then_inc(g_sems["dst_ready"], 1)
                        dve.wait_ge(g_sems["dst_ready"], c + 1 + layer * EC)
                        dve.tensor_scalar(g_onehot[:, :], g_iota[:, :], g_dst[:, 0:1], None, ALU.is_equal)\
                           .then_inc(g_sems[f"oh_ready{layer}"], 1)
                    dve.wait_ge(g_sems["acc_done"], layer + 1)
                    for b in range(NBANK):
                        n = min(BANK_GROUPS, G - b * BANK_GROUPS)
                        ins = dve.tensor_copy(g_sum[:, b * BANK_GROUPS:b * BANK_GROUPS + n, :],
                                              g_acc[b][0:Q, 0:n * MW].rearrange("p (g m) -> p g m", m=MW))
                    ins.then_inc(g_sems["sum_ready"], 1)
                    dve.wait_ge(g_sems["sum_ready"], layer + 1)
                    if layer == 0:
                        with dve.Fori(0, G) as g:
                            dve.wait_ge(g_sems["base_ready"], g + 1)
                            dve.tensor_scalar(g_v[:, 0:1], g_sum[:, bass.ds(g, 1), C + 1], 1.0, None, ALU.add)\
                               .then_inc(g_sems["u_ready"], 1)
                            dve.tensor_copy(g_v[:, 1:2], g_sum[:, bass.ds(g, 1), C])
                            dve.tensor_tensor(u[:, 0:C].unsqueeze(1), g_sum[:, bass.ds(g, 1), 0:C],
                                              x_nat[:, bass.ds(g, 1), :], ALU.add)
                            dve.wait_ge(g_sems["u_ready"], 2 * g + 1)
                            dve.tensor_scalar(u[:, C:2 * C].unsqueeze(1), x_nat[:, bass.ds(g, 1), :], g_v[:, 0:1], None, ALU.mult)\
                               .then_inc(g_sems["u_ready"], 1)
                            dve.wait_ge(g_sems["zs_ready"], g + 1)
                            dve.scalar_tensor_tensor(out=t1[:, :], in0=dense[0:Q, C:2 * C], scalar=g_v[:, 0:1],
                                                     in1=zs[:, 0:C], op0=ALU.mult, op1=ALU.add).then_inc(g_sems["t1_ready"], 1)
                dve.wait_ge(g_sems["base_ready"], G + 1)
                bc = lambda t: t[:, :].unsqueeze(2).broadcast_to([Q, G, C])
                link(dve.tensor_tensor(go[:, :, :], g_sum[:, :, 0:C], base[:, :, :], ALU.add))
                link(dve.tensor_scalar(go[:, :, :], go[:, :, :], 0.0, None, ALU.max))
                link(dve.tensor_reduce(gm[:, :], go[:, :, :], AX.X, ALU.max))
                link(dve.tensor_tensor(go[:, :, :], go[:, :, :], bc(gm), ALU.subtract))
                dve.wait_ge(g_sems["fin_act"], 1)
                link(dve.tensor_reduce(gs[:, :], ge[:, :, :], AX.X, ALU.add))
                dve.wait_ge(g_sems["fin_act"], 2)
                link(dve.tensor_tensor(go[:, :, :], go[:, :, :], bc(gw), ALU.subtract))
                link(dve.tensor_tensor(go[:, :, :], go[:, :, :], x_nat[:, :, :], ALU.add))
                link(dve.tensor_reduce(gm[:, :], go[:, :, :], AX.X, ALU.add))
                link(dve.tensor_scalar(gm[:, :], gm[:, :], 1.0 / C, None, ALU.mult))
                link(dve.tensor_tensor(go[:, :, :], go[:, :, :], bc(gm), ALU.subtract))
                dve.wait_ge(g_sems["fin_act"], 3)
                link(dve.tensor_reduce(gs[:, :], ge[:, :, :], AX.X, ALU.add))
                dve.wait_ge(g_sems["fin_act"], 4)
                link(dve.reciprocal(gm[:, :], gw[:, :]))
                link(dve.tensor_tensor(ge[:, :, :], go[:, :, :], bc(gm), ALU.mult))

        @block.scalar
        def _(act):
            act.wait_ge(xlo_in, 16)
            act.activation(x3[:, :, 0:C], x_lo, ACT.Copy).then_inc(xs_act, 1)
            act.wait_ge(xs_dve, 1)
            act.activation(x3[:, :, C:2 * C], x_rest, ACT.Copy).then_inc(xs_act, 1)
            for j in range(J):
                bank = (acc, dense)[j % 2]
                act.wait_ge(keyt_done, j + 1)
                for t, key in enumerate((keyl, keyr)):
                    src = bank[:, t * Q:(t + 1) * Q].rearrange("p (g k) -> p g k", g=5)
                    act.activation(key[:, 5 * j:5 * j + 5, 0:9], src[:, :, 0:9], ACT.Copy)
                    ins = act.activation(key[:, 5 * j:5 * j + 5, 10:26], src[:, :, 9:25], ACT.Copy)
                ins.then_inc(keys_ready, 1)

            def evacuate(g, s):
                act.wait_ge(built[s], g + 1)
                if s == 3:
                    w0 = SINGLE * WD
                    act.activation(adj4[:, g, :, w0:w0 + WD],
                                   dense[:, 0:G * WD].rearrange("p (h e) -> p h e", h=G), ACT.Copy)\
                       .then_inc(evac[3], 1)
                else:
                    w0 = SETS[s][0] * WD
                    act.activation(adj4[:, g, :, w0:w0 + 8 * WD].rearrange("p h (b e) -> p b h e", b=2),
                                   pset[s][:, :, 0:4 * WD * G].rearrange("p b (h e) -> p b h e", h=G), ACT.Copy)\
                       .then_inc(evac[s], 1)

            for g in range(-1, G + 1):
                h = g - 1
                b = g + 1 < G
                if b:
                    evacuate(g + 1, 3)
                    evacuate(g + 1, 0)
                if h >= 0:
                    act.wait_ge(t_ready, h + 1)
                    act.activation(ut[:, :], dense[:, 0:Q], ACT.Copy)
                    act.activation(vt[:, :], dense[0:2, Q:2 * Q], ACT.Copy).then_inc(ut_ready, 1)
                if b:
                    evacuate(g + 1, 1)
                if h >= 0:
                    act.wait_ge(h_ready, h + 1)
                    act.activation(ht[:, :], dense[:, 256:256 + Q], ACT.Relu).then_inc(ht_ready, 1)
                if b:
                    evacuate(g + 1, 2)
                if h >= 0:
                    act.wait_ge(zp_ready, h + 1)
                    if h >= 1:
                        act.wait_ge(z3_ready, h)
                    act.activation(zs[:, :], dense[0:Q, 0:3 * C], ACT.Copy).then_inc(zs_ready, 1)
            per = 0
            for i, (a, b) in enumerate(BATCHES):
                n = b - a
                act.wait_ge(fch, per + 4)
                act.activation(f_e[:, 0:n, :], f_o[:, 0:n, :], ACT.Exp).then_inc(fact, 1)
                act.wait_ge(fch, per + 5)
                act.activation(f_l[:, 0:n], f_s[:, 0:n], ACT.Ln).then_inc(fact, 1)
                act.wait_ge(fch, per + 9)
                act.activation(f_s[:, 0:n], f_mv[:, 0:n, 1], ACT.Sqrt, bias=EPS).then_inc(fact, 1)
                per += 11

            act.wait_ge(flag_ready, 1)
            act.wait_ge(o_out[0], 16 * ((len(BATCHES) + 1) // 2))
            act.wait_ge(o_out[1], 16 * (len(BATCHES) // 2))
            missed = act.value_load(flag[0:1, 0:1], min_val=0, max_val=1)
            with act.If(missed):
                with act.Fori(0, G) as g:
                    act.wait_ge(g_sems["t_ready"], g + 1)
                    act.activation(ut[:, :], dense[:, 0:Q], ACT.Copy)
                    act.activation(vt[:, :], dense[0:2, Q:2 * Q], ACT.Copy).then_inc(g_sems["ut_ready"], 1)
                    act.wait_ge(g_sems["h_ready"], g + 1)
                    act.activation(ht[:, :], dense[:, 256:256 + Q], ACT.Relu).then_inc(g_sems["ht_ready"], 1)
                    act.wait_ge(g_sems["zp_ready"], g + 1)
                    act.wait_ge(g_sems["base_ready"], g + 1)
                    act.wait_ge(g_sems["z_stored"], 16 * (g + 1))
                    act.activation(zs[:, :], dense[0:Q, 0:3 * C], ACT.Copy).then_inc(g_sems["zs_ready"], 1)
                act.wait_ge(g_sems["fin"], 4)
                act.activation(ge[:, :, :], go[:, :, :], ACT.Exp).then_inc(g_sems["fin_act"], 1)
                act.wait_ge(g_sems["fin"], 5)
                act.activation(gw[:, :], gs[:, :], ACT.Ln).then_inc(g_sems["fin_act"], 1)
                act.wait_ge(g_sems["fin"], 10)
                act.activation(ge[:, :, :], go[:, :, :], ACT.Square).then_inc(g_sems["fin_act"], 1)
                act.wait_ge(g_sems["fin"], 11)
                act.activation(gw[:, :], gs[:, :], ACT.Sqrt, scale=1.0 / C, bias=EPS).then_inc(g_sems["fin_act"], 1)

        @block.tensor
        def _(pe):
            pe.wait_ge(consts, 3)
            pe.wait_ge(sampb_ready, 1)
            pe.matmul(acc[0:Q, 0:Q], samp_b, ident[0:Q, 0:Q], start=True, stop=True).then_inc(sampm_ready, 1)
            pe.wait_ge(rowidx_ready, 1)
            for j in range(J):
                bank = (acc, dense)[j % 2]
                pe.wait_ge(key_ready, j + 1)
                if j >= 2:
                    pe.wait_ge(keys_ready, j - 1)
                pe.transpose(bank[:, 0:Q], lo_f[:, j, :], ident[0:Q, 0:Q])
                pe.transpose(bank[:, Q:2 * Q], key_f[:, j, :], ident[0:Q, 0:Q]).then_inc(keyt_done, 1)
            pe.wait_ge(keys_ready, J)

            def build(g, s):
                if g >= 1:
                    pe.wait_ge(evac[s], g)
                pe.wait_ge(oh_ready[s], g + 1)
                for i in range(8):
                    ins = pe.matmul(
                        pset[s][:, i // 4, 0:4 * WD * G].rearrange("p (h e) -> p h e", h=G)[:, :, i % 4 * WD:(i % 4 + 1) * WD],
                        ohl[s][:, i // 2, :, i % 2], ohr[s][:, i // 2, :, i % 2], start=True, stop=True)
                ins.then_inc(built[s], 1)

            def build_single(g):
                pe.wait_ge(oh_ready[0], g + 1)
                if g >= 3:
                    pe.wait_ge(zs_ready, g - 2)
                elif g >= 1:
                    pe.wait_ge(evac[3], g)
                pe.matmul(dense[:, 0:G * WD], ohl[0][:, 4, :, 0], ohr[0][:, 4, :, 0], start=True, stop=True)\
                  .then_inc(built[3], 1)

            def layer1(g, h0, h1):
                if h0 == 0:
                    pe.wait_ge(evac[2], g + 1)
                    if g >= 1:
                        pe.wait_ge(acc_read, g)
                for h in range(h0, h1):
                    ins = pe.matmul(acc[0:Q, 0:PW + 1], adj4[0:LO, g, h, :], x3[:, h, :],
                                    start=(h == 0), stop=(h == G - 1))
                if h1 == G:
                    ins.then_inc(acc_done, 1)

            for g in range(-1, G + 1):
                h = g - 1
                b, l, d = g + 1 < G, 0 <= g < G, h >= 0
                if g == 0:
                    pe.wait_ge(xs_dve, 2)
                    pe.wait_ge(w_in, 16 * 8)
                if b:
                    build_single(g + 1)
                    build(g + 1, 0)
                if l:
                    layer1(g, 0, 8)
                if d:
                    pe.wait_ge(u_ready, h + 1)
                    if h + 2 < G:
                        pe.wait_ge(evac[3], h + 3)
                    else:
                        pe.wait_ge(zs_ready, h)
                    pe.transpose(dense[:, 0:Q], u[:, :], ident[0:Q, 0:Q])
                    pe.transpose(dense[0:2, Q:2 * Q], stats[:, h, :], ident[0:Q, 0:Q]).then_inc(t_ready, 1)
                if b:
                    build(g + 1, 1)
                if l:
                    layer1(g, 8, 16)
                if d:
                    pe.wait_ge(ut_ready, h + 1)
                    pe.matmul(dense[:, 256:256 + Q], w1c[:, :], ut[:, :], start=True, stop=False)
                    pe.matmul(dense[:, 256:256 + Q], bw1[:, :], vt[:, :], start=False, stop=True).then_inc(h_ready, 1)
                if b:
                    build(g + 1, 2)
                if l:
                    layer1(g, 16, G)
                if d:
                    pe.wait_ge(ht_ready, h + 1)
                    pe.matmul(dense[0:Q, 0:2 * C], ht[:, :], w2c[:, :], start=True, stop=True)
                    pe.matmul(dense[0:Q, 2 * C:3 * C], vt[:, :], bw2[:, :], start=True, stop=True).then_inc(zp_ready, 1)

            pe.wait_ge(z_in, 16)
            for g in range(G):
                if g >= 6:
                    pe.wait_ge(acc2_read, g - 5)
                for h in range(G):
                    ins = pe.matmul(bank2(g)[0:Q, :], adj4[0:LO, g, h, :], z3[:, h, :],
                                    start=(h == 0), stop=(h == G - 1))
                ins.then_inc(acc2_done, 1)
                if g == BATCHES[0][1]:
                    pe.wait_ge(deg_ready, 1)
                    pe.wait_ge(zs_ready, G)
                    pe.matmul(dense[0:1, 0:1], deg_sum[:, :], ones_f[:, :], start=True, stop=True).then_inc(degs_ready, 1)

            pe.wait_ge(flag_ready, 1)
            pe.wait_ge(o_out[0], 16 * ((len(BATCHES) + 1) // 2))
            pe.wait_ge(o_out[1], 16 * (len(BATCHES) // 2))
            missed = pe.value_load(flag[0:1, 0:1], min_val=0, max_val=1)
            with pe.If(missed):
                pe.wait_ge(g_sems["consts"], 3)
                for layer in range(2):
                    if layer:
                        pe.wait_ge(g_sems["sum_ready"], 1)
                    for b in range(NBANK):
                        ins = pe.matmul(g_acc[b][:, :], g_zero[:, 0:128], g_zero[:, :], start=True, stop=False)
                    ins.then_inc(g_sems[f"chunk_done{layer}"], 1)
                    with pe.Fori(0, EC) as c:
                        pe.wait_ge(g_sems[f"gathered{layer}"], 16 * (c + 1))
                        pe.wait_ge(g_sems[f"attr_ready{layer}"], c + 1)
                        pe.wait_ge(g_sems[f"oh_ready{layer}"], c + 1)
                        for g in range(G):
                            b, n = divmod(g, BANK_GROUPS)
                            ins = pe.matmul(g_acc[b][0:Q, n * MW:(n + 1) * MW], g_onehot[:, g * Q:(g + 1) * Q],
                                            g_msg[:, :], start=False, stop=False)
                        ins.then_inc(g_sems[f"chunk_done{layer}"], 1)
                    for b in range(NBANK):
                        ins = pe.matmul(g_acc[b][:, :], g_zero[:, 0:128], g_zero[:, :], start=False, stop=True)
                    ins.then_inc(g_sems["acc_done"], 1)
                    if layer == 0:
                        with pe.Fori(0, G) as g:
                            pe.wait_ge(g_sems["u_ready"], 2 * g + 2)
                            pe.transpose(dense[:, 0:Q], u[:, :], ident[0:Q, 0:Q])
                            pe.transpose(dense[0:2, Q:2 * Q], g_v[:, :], ident[0:Q, 0:Q]).then_inc(g_sems["t_ready"], 1)
                            pe.wait_ge(g_sems["ut_ready"], g + 1)
                            pe.matmul(dense[:, 256:256 + Q], w1c[:, :], ut[:, :], start=True, stop=False)
                            pe.matmul(dense[:, 256:256 + Q], bw1[:, :], vt[:, :], start=False, stop=True).then_inc(g_sems["h_ready"], 1)
                            pe.wait_ge(g_sems["ht_ready"], g + 1)
                            pe.matmul(dense[0:Q, 0:2 * C], ht[:, :], w2c[:, :], start=True, stop=True)
                            pe.matmul(dense[0:Q, 2 * C:3 * C], vt[:, :], bw2[:, :], start=True, stop=True).then_inc(g_sems["zp_ready"], 1)


def kernel(x, src, dst, edge_weight1, L0_gnn_W1, L0_gnn_b1, L0_gnn_W2, L0_gnn_b2):
    import numpy as _np
    import concourse.bacc as _bacc
    from concourse import mybir as _mybir
    from concourse.bass_utils import run_bass_kernel_spmd as _run

    nc = _bacc.Bacc("TRN2", target_bir_lowering=False, num_devices=1)
    E = src.shape[0]
    arrays, args = {}, []
    edges = _np.stack([_np.asarray(src), _np.asarray(dst)], axis=1)
    edges = _np.concatenate([edges, _np.full((128, 2), N, edges.dtype)], axis=0)
    dst_rows = _np.asarray(dst).reshape(Q, -1)
    attr = _np.concatenate([_np.asarray(edge_weight1)[:, 0], _np.zeros(128, _np.float32)])[:, None]
    for name, a in (("x", x), ("dst", dst_rows), ("edges", edges), ("edge_attr", attr), ("W1", L0_gnn_W1), ("b1", L0_gnn_b1),
                    ("W2", L0_gnn_W2), ("b2", L0_gnn_b2)):
        a = _np.ascontiguousarray(a)
        arrays[f"in_{name}"] = a
        args.append(nc.dram_tensor(f"in_{name}", a.shape, _mybir.dt.from_np(a.dtype), kind="ExternalInput").ap())
    out = nc.dram_tensor("out_0", [N, C], _mybir.dt.float32, kind="ExternalOutput").ap()
    gnn(nc, *args, out, E)
    r = _run(nc, [arrays], core_ids=[0])
    return r.results[0]["out_0"]
```

```python
import concourse.bass as bass
from concourse import mybir
from contextlib import ExitStack

FP32 = mybir.dt.float32
BF16 = mybir.dt.bfloat16
I32 = mybir.dt.int32
ALU = mybir.AluOpType
ACT = mybir.ActivationFunctionType
AX = mybir.AxisListType

N = 3125
C = 64
HID = 128
Q = 125
G = N // Q
EPS = 1e-5

SLOTS = 128
WD = 5
K = N // WD
J = K // Q
PW = 3 * C
XC = C + 1
XW = 3 * XC
SETS = ((0, 8, 0), (9, 8, 10), (17, 8, 18))
SINGLE = 8
KW = 26
KB = 12
ROUND = 12582912.0
BATCHES = ((0, 6), (6, 12), (12, 16), (16, 19), (19, 22), (22, 25))


def gnn(nc, x, dst, edges, edge_attr, W1, b1, W2, b2, out, E):
    EC = E // Q
    BG = max(b - a for a, b in BATCHES)

    with ExitStack() as ctx:
        def sb(name, shape, dt):
            return ctx.enter_context(nc.sbuf_tensor(name, shape, dt))

        def pb(name, shape, dt):
            return ctx.enter_context(nc.psum_tensor(name, shape, dt))

        def sem(name):
            return ctx.enter_context(nc.semaphore(name))

        se_dram = nc.dram_tensor("se_scratch", [N], FP32, kind="Internal").ap()

        w1c = sb("w1c", [128, HID], FP32)
        bmask = sb("bmask", [KB, 3], FP32)
        bw = sb("bw", [KB, HID + C], BF16)
        w2c = sb("w2c", [HID, 2 * C], FP32)
        ident = sb("ident", [128, 128], FP32)
        ident16 = sb("ident16", [128, Q], BF16)
        iota2 = sb("iota2", [128, SLOTS, 2], BF16)
        thr = sb("thr", [Q, J], FP32)
        x_nat = sb("x_nat", [Q, G, C], FP32)
        base = sb("base", [Q, G, C], FP32)
        deg = sb("deg", [Q, G], FP32)
        se = sb("se", [Q, G], FP32)
        se_rest = sb("se_rest", [Q, G, 2], FP32)
        stats = sb("stats", [Q, G, KB], BF16)

        adj = sb("adj", [128, G * G * Q + 1], BF16)
        adj4 = adj[:, 0:G * G * Q].rearrange("p (g h e) -> p g h e", g=G, h=G)
        free = [G * G * Q]

        def tail(shape, dt):
            n = 1
            for s in shape[1:]:
                n *= s
            n *= 2 if dt in (FP32, I32) else 1
            free[0] -= n + n % 2
            ap = adj[0:shape[0], free[0] - free[0] % 2:free[0] - free[0] % 2 + n]
            free[0] -= free[0] % 2
            if dt is not BF16:
                ap = ap.bitcast(dt)
            if len(shape) == 3:
                ap = ap.rearrange("p (a b) -> p a b", a=shape[1])
            return ap

        se_w = tail([Q, J, WD], FP32)
        se_junk = tail([Q, J * WD, SLOTS], BF16)
        attrs = tail([Q, J, SLOTS], FP32)
        d_f = tail([Q, J, SLOTS], FP32)
        sums_group = free[0] // (G * Q)
        x_rest = tail([Q, G, C], FP32)
        samp = tail([Q, 1], I32)
        ones = tail([Q, EC], BF16)
        brows = tail([KB, HID + C], FP32)
        brest = tail([KB, 2, HID + C], FP32)
        bpart = tail([KB, 3, HID + C], BF16)
        samp_b = tail([Q, Q], FP32)
        junk = tail([Q, J, EC], BF16)
        cnt1 = tail([Q, J], FP32)
        cnt2 = tail([Q, J], FP32)
        row_idx = tail([Q, J], I32)
        off_idx = tail([Q, J], I32)
        rows = tail([Q, J, EC], I32)
        pairs = tail([Q, J, 2 * SLOTS], I32)
        hi_q = tail([Q, J, SLOTS], FP32)
        lo_f = tail([Q, J, SLOTS], FP32)
        hi_f = tail([Q, J, SLOTS], FP32)
        w_f = tail([Q, J, SLOTS], FP32)
        p_f = tail([Q, J, SLOTS], FP32)
        m_f = tail([Q, J, SLOTS], FP32)
        key_f = tail([Q, J, SLOTS], FP32)
        assert free[0] // (G * Q) > 5 and sums_group > 5 * (J - 1) + 2

        keyl = sb("keyl", [128, G, KW], BF16)
        keyr = sb("keyr", [128, G, KW], BF16)
        ohl = [sb(f"ohl{s}", [128, 5 if s == 0 else 4, Q, 2], BF16) for s in range(3)]
        ohr = [sb(f"ohr{s}", [128, 5 if s == 0 else 4, G * WD, 2], BF16) for s in range(3)]
        x3_flat = sb("x3", [Q, G * XW + 1], BF16)
        x3 = x3_flat[:, 0:G * XW].rearrange("p (g c) -> p g c", g=G)
        z3 = sb("z3", [Q, G, PW], BF16)

        s_sum = sb("s_sum", [Q, XC], FP32)
        u = sb("u", [Q, 2 * C], FP32)
        ut = sb("ut", [2 * C, Q], FP32)
        vt = sb("vt", [KB, Q], BF16)
        ht = sb("ht", [HID, Q], FP32)
        zs = sb("zs", [Q, 3 * C], FP32)
        zr = sb("zr", [Q, C], FP32)
        t1 = sb("t1", [Q, C], FP32)
        t2 = sb("t2", [Q, C], FP32)

        used = [0]

        def late(shape):
            n = 2
            for d in shape[1:]:
                n *= d
            ap = x3_flat[:, used[0]:used[0] + n].bitcast(FP32)
            used[0] += n
            if len(shape) == 3:
                ap = ap.rearrange("p (a b) -> p a b", a=shape[1])
            return ap

        f_o = late([Q, BG, C])
        f_p = late([Q, BG, C])
        f_e = late([Q, BG, C])
        f_v = [late([Q, BG, C]) for _ in range(2)]
        f_m = late([Q, BG])
        f_s = late([Q, BG])
        f_l = late([Q, BG])
        f_bn = late([Q, BG, 6])
        f_mv = late([Q, BG, 2])
        f_g = late([Q, BG])
        f_y = late([Q, BG])
        f_r = late([Q, BG])
        f_var = late([Q, BG])
        f_mean = late([Q, BG])
        assert used[0] <= G * XW

        pset = [pb(f"pset{s}", [128, 2, 512], FP32) for s in range(3)]
        acc = pb("acc", [128, 512], FP32)
        dense = pb("dense", [128, 512], FP32)

        def bank2(g):
            return pset[(g // 2) % 3][:, g % 2, 0:PW]

        MW = C + 2
        BANK_GROUPS = 512 // MW
        NBANK = -(-G // BANK_GROUPS)
        gz_dram = nc.dram_tensor("gz_scratch", [N, C], FP32, kind="Internal").ap()
        deg_sum = sb("deg_sum", [Q, 1], FP32)
        ones_f = sb("ones_f", [Q, 1], FP32)
        flag = sb("flag", [1, 1], I32)
        free[0] = G * G * Q
        g_edges = tail([Q, EC, 2], I32)
        g_attr = tail([Q, EC], FP32)
        g_iota = tail([Q, N], FP32)
        g_onehot = tail([Q, N], FP32)
        g_idx = tail([Q, 1], I32)
        g_msg = tail([Q, MW], FP32)
        g_dst = tail([Q, 1], FP32)
        g_free = tail([1, 2], FP32)
        g_zero = tail([1, 512], FP32)
        g_sum = tail([Q, G, MW], FP32)
        g_v = tail([Q, 2], FP32)
        go = tail([Q, G, C], FP32)
        ge = tail([Q, G, C], FP32)
        gm = tail([Q, G], FP32)
        gs = tail([Q, G], FP32)
        gw = tail([Q, G], FP32)
        g_bw1 = tail([2, HID], FP32)
        g_bw2 = tail([2, C], FP32)
        g_vt = tail([2, Q], FP32)
        g_acc = [pset[b // 2][:, b % 2, :] for b in range(NBANK)]
        assert free[0] >= 0
        deg_ready = sem("deg_ready")
        degs_ready = sem("degs_ready")
        flag_ready = sem("flag_ready")
        g_sems = {n: sem("g_" + n) for n in (
            "loaded", "consts", "idx_ready", "attr_ready0", "attr_ready1", "gathered0", "gathered1",
            "oh_ready0", "oh_ready1", "chunk_done0", "chunk_done1", "dst_ready", "acc_done", "sum_ready",
            "u_ready", "t_ready", "ut_ready", "h_ready", "ht_ready", "zp_ready", "zs_ready", "t1_ready",
            "base_ready", "z_stored", "fin", "fin_act", "out_stored")}

        samp_in = sem("samp_in")
        w_in = sem("w_in")
        b_in = sem("b_in")
        xnat_in = sem("xnat_in")
        rows_in = [sem(f"rows_in{j}") for j in range(J)]
        pairs_in = [sem(f"pairs_in{j}") for j in range(J)]
        attrs_in = [sem(f"attrs_in{j}") for j in range(J)]
        se_out = [sem(f"se_out{j}") for j in range(J)]
        se_in = [sem(f"se_in{j}") for j in range(J)]
        o_out = [sem("o_out0"), sem("o_out1")]
        consts = sem("consts")
        sampb_ready = sem("sampb_ready")
        sampm_ready = sem("sampm_ready")
        rowidx_ready = sem("rowidx_ready")
        off_ready = sem("off_ready")
        key_ready = sem("key_ready")
        keyt_done = sem("keyt_done")
        keys_ready = sem("keys_ready")
        xs_rest = sem("xs_rest")
        xs_ready = sem("xs_ready")
        bchain = sem("bias_chain")
        bw_ready = sem("bw_ready")
        sech = sem("se_chain")
        se_parts = sem("se_parts")
        se_ready = sem("se_ready")
        dch = sem("dve_chain")
        oh_ready = [sem(f"oh_ready{s}") for s in range(3)]
        built = [sem(f"built{s}") for s in range(4)]
        evac = [sem(f"evac{s}") for s in range(4)]
        acc_done = sem("acc_done")
        acc_read = sem("acc_read")
        deg_done = sem("deg_done")
        u_ready = sem("u_ready")
        t_ready = sem("t_ready")
        ut_ready = sem("ut_ready")
        h_ready = sem("h_ready")
        ht_ready = sem("ht_ready")
        zp_ready = sem("zp_ready")
        zs_ready = sem("zs_ready")
        z3_ready = sem("z3_ready")
        base_ready = sem("base_ready")
        pch = sem("pool_chain")
        acc2_done = sem("acc2_done")
        acc2_read = sem("acc2_read")
        fch = sem("final_chain")
        fact = sem("final_act")

        at = {}

        block = ctx.enter_context(nc.Block())

        @block.gpsimd
        def _(gp):
            gp.memset(ident[:, :], 0.0).then_inc(consts, 1)
            gp.iota(thr[:, :], [[Q * WD, J]], base=0, channel_multiplier=WD,
                    allow_small_or_imprecise_dtypes=True).then_inc(consts, 1)
            gp.wait_ge(consts, 2)
            gp.affine_select(out=ident[:, :], in_=ident[:, :], compare_op=ALU.not_equal, fill=1.0,
                             base=0, pattern=[[-1, 128]], channel_multiplier=1).then_inc(consts, 1)
            gp.memset(ones[:, :], 1.0).then_inc(consts, 1)
            gp.wait_ge(consts, 4)
            gp.tensor_copy(ident16[:, :], ident[:, 0:Q]).then_inc(consts, 1)
            gp.memset(ones_f[:, :], 1.0)
            gp.iota(iota2[:, :, :], [[1, SLOTS], [0, 2]], base=0, channel_multiplier=0,
                    allow_small_or_imprecise_dtypes=True).then_inc(consts, 1)
            gp.memset(keyl[:, :, SINGLE + 1:SINGLE + 2], 0.0).then_inc(consts, 1)
            gp.memset(keyr[:, :, SINGLE + 1:SINGLE + 2], 0.0).then_inc(consts, 1)
            gp.memset(x3[:, :, C:XC], 1.0).then_inc(consts, 1)
            gp.memset(x3[:, :, XC + C:2 * XC], 0.0).then_inc(consts, 1)
            gp.memset(x3[:, :, 2 * XC + C:3 * XC], 0.0).then_inc(consts, 1)
            gp.wait_ge(rowidx_ready, 1)

            def gather_rows(j):
                gp.indirect_dma_start(rows[:, j, :], None, dst,
                                      bass.IndirectOffsetOnAxis(row_idx[:, j:j + 1], 0)).then_inc(rows_in[j], 16)

            def gather_edges(j):
                gp.wait_ge(off_ready, j + 1)
                gp.indirect_dma_start(pairs[:, j, :], None, edges,
                                      bass.IndirectOffsetOnAxis(off_idx[:, j:j + 1], 0)).then_inc(pairs_in[j], 16)

            def gather_attrs(j):
                gp.indirect_dma_start(attrs[:, j, :], None, edge_attr,
                                      bass.IndirectOffsetOnAxis(off_idx[:, j:j + 1], 0)).then_inc(attrs_in[j], 16)

            for j in range(4):
                gather_rows(j)
            gather_edges(0)
            gather_rows(4)
            gather_attrs(0)
            for j in range(1, J):
                gather_edges(j)
            gp.wait_ge(xs_ready, 1)
            gp.tensor_tensor(x_rest, x_nat[:, :, :], x3[:, :, 0:C], ALU.subtract).then_inc(xs_rest, 1)
            for j in range(1, 3):
                gather_attrs(j)
            gp.wait_ge(xs_ready, 2)
            gp.tensor_tensor(x3[:, :, 2 * XC:2 * XC + C], x_rest, x3[:, :, XC:XC + C], ALU.subtract).then_inc(xs_ready, 1)
            for j in range(3, J):
                gather_attrs(j)
            gp.wait_ge(xnat_in, 16)

            def split_sums(j):
                s0, s1, s2 = (stats[:, 5 * j:5 * j + 5, 3 + 3 * k:6 + 3 * k] for k in range(3))
                v = se[:, 5 * j:5 * j + 5]
                r = se_rest[:, 5 * j:5 * j + 5, :]
                wide = [Q, 5, 3]
                gp.wait_ge(se_in[j], 16)
                gp.tensor_copy(s0, v.unsqueeze(2).broadcast_to(wide)).then_inc(sech, 1)
                gp.wait_ge(sech, 4 * j + 1)
                gp.tensor_tensor(r[:, :, 0], v, s0[:, :, 0], ALU.subtract).then_inc(sech, 1)
                gp.wait_ge(sech, 4 * j + 2)
                gp.tensor_copy(s1, r[:, :, 0:1].broadcast_to(wide)).then_inc(sech, 1)
                gp.wait_ge(sech, 4 * j + 3)
                gp.tensor_tensor(r[:, :, 1], r[:, :, 0], s1[:, :, 0], ALU.subtract).then_inc(sech, 1)
                gp.wait_ge(sech, 4 * j + 4)
                gp.tensor_copy(s2, r[:, :, 1:2].broadcast_to(wide)).then_inc(se_parts, 1)

            p0, p1, p2 = (bpart[:, k, :] for k in range(3))
            r0, r1 = brest[:, 0, :], brest[:, 1, :]
            done = [1]

            def blink(ins):
                done[0] += 1
                ins.then_inc(bchain, 1)
                gp.wait_ge(bchain, done[0])

            gp.wait_ge(bchain, 1)
            gp.wait_ge(b_in, 16 * 4)
            blink(gp.tensor_copy(p0, brows))
            blink(gp.tensor_tensor(r0, brows, p0, ALU.subtract))
            blink(gp.tensor_copy(p1, r0))
            blink(gp.tensor_tensor(r1, r0, p1, ALU.subtract))
            gp.tensor_copy(p2, r1).then_inc(bchain, 1)

            split_sums(0)
            n = 0
            for h in range(G + 1):
                if h < G:
                    gp.wait_ge(acc_read, h + 1)
                    if h >= 1:
                        gp.wait_ge(t_ready, h)
                    gp.tensor_scalar(deg[:, h:h + 1], s_sum[:, C:XC], 1.0, None, ALU.add).then_inc(deg_done, 1)
                    gp.tensor_tensor(u[:, 0:C], s_sum[:, 0:C], x_nat[:, h, :], ALU.add)
                    gp.wait_ge(deg_done, h + 1)
                    gp.tensor_copy(stats[:, h, 0:3], deg[:, h:h + 1].broadcast_to([Q, 3]))
                    gp.tensor_tensor(u[:, C:2 * C], x_nat[:, h, :], deg[:, h:h + 1].broadcast_to([Q, C]), ALU.mult).then_inc(u_ready, 1)
                if h == 0:
                    continue
                if h % 5 == 4 and h < G - 1:
                    split_sums(h // 5 + 1)
                d = h - 1
                gp.wait_ge(zs_ready, d + 1)
                gp.tensor_copy(z3[:, d, 0:C], zs[:, 0:C]).then_inc(pch, 1)
                gp.tensor_tensor(t1[:, :], zs[:, C:2 * C], deg[:, d:d + 1].broadcast_to([Q, C]), ALU.mult).then_inc(pch, 1)
                gp.wait_ge(pch, n + 1)
                gp.tensor_tensor(zr[:, :], zs[:, 0:C], z3[:, d, 0:C], ALU.subtract).then_inc(pch, 1)
                gp.wait_ge(pch, n + 2)
                gp.tensor_tensor(t2[:, :], t1[:, :], zs[:, 0:C], ALU.add).then_inc(pch, 1)
                gp.wait_ge(pch, n + 3)
                gp.tensor_copy(z3[:, d, C:2 * C], zr[:, :]).then_inc(pch, 1)
                gp.wait_ge(pch, n + 5)
                gp.tensor_tensor(z3[:, d, 2 * C:3 * C], zr[:, :], z3[:, d, C:2 * C], ALU.subtract).then_inc(z3_ready, 1)
                gp.wait_ge(pch, n + 4)
                gp.tensor_tensor(base[:, d, :], t2[:, :], zs[:, 2 * C:3 * C], ALU.add).then_inc(base_ready, 1)
                n += 5

            gp.wait_ge(flag_ready, 1)
            gp.wait_ge(o_out[0], 16 * ((len(BATCHES) + 1) // 2))
            gp.wait_ge(o_out[1], 16 * (len(BATCHES) // 2))
            missed = gp.value_load(flag[0:1, 0:1], min_val=0, max_val=1)
            with gp.If(missed):
                gp.memset(g_free[:, 0:1], 0.0).then_inc(g_sems["base_ready"], 1)
                gp.memset(g_free[:, 1:2], 0.0).then_inc(g_sems["z_stored"], 16)
                gp.memset(g_zero[:, :], 0.0).then_inc(g_sems["consts"], 1)
                gp.memset(g_msg[:, C + 1:C + 2], 1.0).then_inc(g_sems["consts"], 1)
                gp.iota(g_iota[:, :], [[1, N]], base=0, channel_multiplier=0,
                        allow_small_or_imprecise_dtypes=True).then_inc(g_sems["consts"], 1)
                gp.wait_ge(g_sems["loaded"], 16 * 6)
                for layer, table in ((0, x), (1, gz_dram)):
                    if layer:
                        gp.wait_ge(g_sems["z_stored"], 16 * (G + 1))
                    with gp.Fori(0, EC) as c:
                        gp.wait_ge(g_sems[f"chunk_done{layer}"], c + 1)
                        gp.tensor_copy(g_idx[:, :], g_edges[:, bass.ds(c, 1), 0]).then_inc(g_sems["idx_ready"], 1)
                        gp.wait_ge(g_sems["idx_ready"], c + 1 + layer * EC)
                        gp.tensor_copy(g_msg[:, C:C + 1], g_attr[:, bass.ds(c, 1)]).then_inc(g_sems[f"attr_ready{layer}"], 1)
                        gp.indirect_dma_start(g_msg[:, 0:C], None, table,
                                              bass.IndirectOffsetOnAxis(g_idx[:, 0:1], 0)).then_inc(g_sems[f"gathered{layer}"], 16)
                    if layer == 0:
                        with gp.Fori(0, G) as g:
                            gp.wait_ge(g_sems["t1_ready"], g + 1)
                            gp.tensor_tensor(base[:, bass.ds(g, 1), :], t1[:, :].unsqueeze(1), zs[:, 2 * C:3 * C].unsqueeze(1), ALU.add)\
                              .then_inc(g_sems["base_ready"], 1)

        @block.vector
        def _(dve):
            chain = [0]

            def link(ins):
                chain[0] += 1
                ins.then_inc(dch, 1)
                dve.wait_ge(dch, chain[0])

            dve.wait_ge(samp_in, 16)
            dve.tensor_copy(samp_b, samp.broadcast_to([Q, Q])).then_inc(sampb_ready, 1)
            dve.wait_ge(consts, 3)
            dve.tensor_reduce(bmask[:, :], ident[0:KB, 0:KB].rearrange("p (a b) -> p b a", b=3), AX.X, ALU.add)\
               .then_inc(bchain, 1)
            dve.wait_ge(sampm_ready, 1)
            dve.wait_ge(consts, 4)
            for j in range(J):
                ins = dve.scalar_tensor_tensor(out=junk[:, j, 0:Q], in0=acc[0:Q, 0:Q], scalar=thr[:, j:j + 1],
                                               in1=ones[:, 0:Q], op0=ALU.is_lt, op1=ALU.mult,
                                               accum_out=cnt1[:, j:j + 1])
            link(ins)
            dve.tensor_scalar(row_idx, cnt1, -1.0, 0.0, ALU.add, ALU.max).then_inc(rowidx_ready, 1)
            dve.wait_ge(rowidx_ready, 1)
            def offset(j):
                dve.wait_ge(rows_in[j], 16)
                link(dve.scalar_tensor_tensor(out=junk[:, j, :], in0=rows[:, j, :], scalar=thr[:, j:j + 1],
                                              in1=ones[:, :], op0=ALU.is_lt, op1=ALU.mult,
                                              accum_out=cnt2[:, j:j + 1]))
                dve.scalar_tensor_tensor(out=off_idx[:, j:j + 1], in0=row_idx[:, j:j + 1], scalar=float(EC),
                                         in1=cnt2[:, j:j + 1], op0=ALU.mult, op1=ALU.add).then_inc(off_ready, 1)

            for j in range(J - 1):
                offset(j)

            def keys(a, b):
                for j in range(a, b):
                    dve.wait_ge(pairs_in[j], 16)
                    ins = dve.tensor_scalar(d_f[:, j, :], pairs[:, j, 1::2], thr[:, j:j + 1], None, ALU.subtract)
                srcs = pairs[:, a:b, 0::2]
                dve.tensor_scalar(hi_q[:, a:b, :], srcs, 1.0 / Q, 0.5 / Q - 0.5, ALU.mult, ALU.add)
                link(ins)
                link(dve.scalar_tensor_tensor(out=w_f[:, a:b, :], in0=d_f[:, a:b, :], scalar=-float(WD - 1),
                                              in1=d_f[:, a:b, :], op0=ALU.add, op1=ALU.mult))
                link(dve.tensor_scalar(hi_f[:, a:b, :], hi_q[:, a:b, :], ROUND, ROUND, ALU.add, ALU.subtract))
                dve.tensor_scalar(p_f[:, a:b, :], w_f[:, a:b, :], 0.0, 8192.0, ALU.is_gt, ALU.mult)
                link(dve.scalar_tensor_tensor(out=m_f[:, a:b, :], in0=hi_f[:, a:b, :], scalar=float(WD),
                                              in1=d_f[:, a:b, :], op0=ALU.mult, op1=ALU.add))
                dve.scalar_tensor_tensor(out=lo_f[:, a:b, :], in0=hi_f[:, a:b, :], scalar=-float(Q), in1=srcs,
                                         op0=ALU.mult, op1=ALU.add)
                dve.tensor_tensor(key_f[:, a:b, :], m_f[:, a:b, :], p_f[:, a:b, :], ALU.add).then_inc(key_ready, 1)

            def attr_sums(j, r0, r1):
                dve.wait_ge(attrs_in[j], 16)
                for r in range(r0, r1):
                    dve.scalar_tensor_tensor(out=se_junk[:, j * WD + r, :], in0=d_f[:, j, :], scalar=float(r),
                                             in1=attrs[:, j, :], op0=ALU.is_equal, op1=ALU.mult,
                                             accum_out=se_w[:, j, r:r + 1]).then_inc(se_ready, 1)

            def onehots(g, s):
                w0, n, k0 = SETS[s]
                n = n // 2 + (s == 0)
                if g >= 1:
                    dve.wait_ge(built[s], g)
                    if s == 0:
                        dve.wait_ge(built[3], g)
                for oh, key in ((ohl, keyl), (ohr, keyr)):
                    ins = dve.tensor_tensor(
                        out=oh[s][:, :, :, :],
                        in0=iota2[:, 0:Q, :].unsqueeze(1).broadcast_to([128, n, Q, 2]),
                        in1=key[:, g, k0:k0 + 2 * n].rearrange("p (q o k) -> p q o k", o=1, k=2)
                        .broadcast_to([128, n, Q, 2]),
                        op=ALU.is_equal)
                ins.then_inc(oh_ready[s], 1)

            keys(0, 1)
            offset(J - 1)
            dve.wait_ge(consts, 11)
            dve.wait_ge(keys_ready, 1)
            for s in range(3):
                onehots(0, s)
            for s in range(3):
                onehots(1, s)
            attr_sums(0, 0, WD)
            keys(1, J)
            for s in range(2):
                onehots(2, s)
            for h in range(G):
                dve.wait_ge(acc_done, h + 1)
                if h >= 1:
                    dve.wait_ge(u_ready, h)
                dve.tensor_reduce(s_sum[:, :], acc[0:Q, 0:XW].rearrange("p (t c) -> p c t", t=3), AX.X, ALU.add)\
                   .then_inc(acc_read, 1)
                if h + 2 < G:
                    onehots(h + 2, 2)
                if h == 0:
                    dve.wait_ge(bchain, 6)
                    r0, r1 = brest[:, 0, :], brest[:, 1, :]
                    link(dve.tensor_scalar(r0, bpart[:, 0, :], bmask[:, 0:1], None, ALU.mult))
                    link(dve.scalar_tensor_tensor(out=r1, in0=bpart[:, 1, :], scalar=bmask[:, 1:2], in1=r0,
                                                  op0=ALU.mult, op1=ALU.add))
                    dve.scalar_tensor_tensor(out=bw[:, :], in0=bpart[:, 2, :], scalar=bmask[:, 2:3], in1=r1,
                                             op0=ALU.mult, op1=ALU.add).then_inc(bw_ready, 1)
                if h + 3 == 5:
                    dve.wait_ge(keys_ready, 3)
                if h + 3 < G:
                    onehots(h + 3, 0)
                    onehots(h + 3, 1)
                if h // 5 + 1 < J and h % 5 < 3:
                    attr_sums(h // 5 + 1, 2 * (h % 5), min(2 * (h % 5) + 2, WD))

            dve.wait_ge(deg_done, G)
            dve.tensor_reduce(deg_sum[:, :], deg[:, :], AX.X, ALU.add).then_inc(deg_ready, 1)

            fc = [0]

            def fpost(ins):
                fc[0] += 1
                ins.then_inc(fch, 1)

            def flink(ins):
                fpost(ins)
                dve.wait_ge(fch, fc[0])

            na = 0
            for i, (a, b) in enumerate(BATCHES):
                n = b - a
                o, p, e, vv = f_o[:, 0:n, :], f_p[:, 0:n, :], f_e[:, 0:n, :], f_v[i % 2][:, 0:n, :]

                def bc(t):
                    return t[:, 0:n].unsqueeze(2).broadcast_to([Q, n, C])

                for g in range(a, b):
                    dve.wait_ge(acc2_done, g + 1)
                    dve.tensor_reduce(f_o[:, g - a, :], bank2(g)[0:Q, :].rearrange("p (t c) -> p c t", t=3),
                                      AX.X, ALU.add).then_inc(acc2_read, 1)
                dve.wait_ge(acc2_read, b)
                if i == 0:
                    dve.wait_ge(base_ready, G)
                m, total, log, var, mean, y, r = (t[:, 0:n] for t in (f_m, f_s, f_l, f_var, f_mean, f_y, f_r))
                flink(dve.tensor_tensor(p, o, base[:, a:b, :], ALU.add))
                flink(dve.tensor_reduce(m, p, AX.X, ALU.max))
                flink(dve.tensor_scalar(m, m, 0.0, None, ALU.max))
                flink(dve.scalar_tensor_tensor(out=o, in0=p, scalar=0.0, in1=bc(f_m), op0=ALU.max, op1=ALU.subtract))
                at["shifted", i] = fc[0]
                flink(dve.tensor_tensor(p, o, x_nat[:, a:b, :], ALU.add))
                dve.wait_ge(fact, na + 1)
                fpost(dve.tensor_reduce(total, e, AX.X, ALU.add))
                at["sums", i] = fc[0]
                for k in range(n):
                    ins = dve.bn_stats(f_bn[:, k, :], p[:, k, :])
                flink(ins)
                for k in range(n):
                    ins = dve.bn_aggr(f_mv[:, k, :], f_bn[:, k, :])
                flink(ins)
                at["variance", i] = fc[0]
                fpost(dve.tensor_scalar(var, f_mv[:, 0:n, 1], EPS, None, ALU.add))
                dve.wait_ge(fact, na + 2)
                fpost(dve.tensor_tensor(mean, f_mv[:, 0:n, 0], log, ALU.subtract))
                flink(dve.tensor_tensor(o, p, bc(f_l), ALU.subtract))
                dve.wait_ge(fact, na + 4)
                fpost(dve.tensor_tensor(m, y, y, ALU.mult))
                flink(dve.tensor_tensor(o, o, bc(f_mean), ALU.subtract))
                flink(dve.scalar_tensor_tensor(out=m, in0=m, scalar=-0.5, in1=var, op0=ALU.mult, op1=ALU.mult))
                flink(dve.scalar_tensor_tensor(out=r, in0=m, scalar=1.5, in1=y, op0=ALU.add, op1=ALU.mult))
                if i >= 2:
                    dve.wait_ge(o_out[i % 2], 16 * (i // 2))
                flink(dve.tensor_tensor(vv, o, bc(f_r), ALU.mult))
                at["stored", i] = fc[0]
                na += 4
                if i == 1:
                    dve.wait_ge(degs_ready, 1)
                    dve.tensor_scalar(flag[:, :], dense[0:1, 0:1], float(E + N), None, ALU.not_equal)\
                       .then_inc(flag_ready, 1)

            dve.wait_ge(flag_ready, 1)
            dve.wait_ge(o_out[0], 16 * ((len(BATCHES) + 1) // 2))
            dve.wait_ge(o_out[1], 16 * (len(BATCHES) // 2))
            missed = dve.value_load(flag[0:1, 0:1], min_val=0, max_val=1)
            with dve.If(missed):
                chain = [0]

                def link(ins):
                    chain[0] += 1
                    ins.then_inc(g_sems["fin"], 1)
                    dve.wait_ge(g_sems["fin"], chain[0])

                dve.wait_ge(g_sems["consts"], 3)
                dve.wait_ge(g_sems["loaded"], 16 * 6)
                for layer in range(2):
                    with dve.Fori(0, EC) as c:
                        dve.wait_ge(g_sems[f"chunk_done{layer}"], c + 1)
                        dve.tensor_copy(g_dst[:, :], g_edges[:, bass.ds(c, 1), 1]).then_inc(g_sems["dst_ready"], 1)
                        dve.wait_ge(g_sems["dst_ready"], c + 1 + layer * EC)
                        dve.tensor_scalar(g_onehot[:, :], g_iota[:, :], g_dst[:, 0:1], None, ALU.is_equal)\
                           .then_inc(g_sems[f"oh_ready{layer}"], 1)
                    dve.wait_ge(g_sems["acc_done"], layer + 1)
                    for b in range(NBANK):
                        n = min(BANK_GROUPS, G - b * BANK_GROUPS)
                        ins = dve.tensor_copy(g_sum[:, b * BANK_GROUPS:b * BANK_GROUPS + n, :],
                                              g_acc[b][0:Q, 0:n * MW].rearrange("p (g m) -> p g m", m=MW))
                    ins.then_inc(g_sems["sum_ready"], 1)
                    dve.wait_ge(g_sems["sum_ready"], layer + 1)
                    if layer == 0:
                        with dve.Fori(0, G) as g:
                            dve.wait_ge(g_sems["base_ready"], g + 1)
                            dve.tensor_scalar(g_v[:, 0:1], g_sum[:, bass.ds(g, 1), C + 1], 1.0, None, ALU.add)\
                               .then_inc(g_sems["u_ready"], 1)
                            dve.tensor_copy(g_v[:, 1:2], g_sum[:, bass.ds(g, 1), C])
                            dve.tensor_tensor(u[:, 0:C].unsqueeze(1), g_sum[:, bass.ds(g, 1), 0:C],
                                              x_nat[:, bass.ds(g, 1), :], ALU.add)
                            dve.wait_ge(g_sems["u_ready"], 2 * g + 1)
                            dve.tensor_scalar(u[:, C:2 * C].unsqueeze(1), x_nat[:, bass.ds(g, 1), :], g_v[:, 0:1], None, ALU.mult)\
                               .then_inc(g_sems["u_ready"], 1)
                            dve.wait_ge(g_sems["zs_ready"], g + 1)
                            dve.scalar_tensor_tensor(out=t1[:, :], in0=dense[0:Q, C:2 * C], scalar=g_v[:, 0:1],
                                                     in1=zs[:, 0:C], op0=ALU.mult, op1=ALU.add).then_inc(g_sems["t1_ready"], 1)
                dve.wait_ge(g_sems["base_ready"], G + 1)
                bc = lambda t: t[:, :].unsqueeze(2).broadcast_to([Q, G, C])
                link(dve.tensor_tensor(go[:, :, :], g_sum[:, :, 0:C], base[:, :, :], ALU.add))
                link(dve.tensor_scalar(go[:, :, :], go[:, :, :], 0.0, None, ALU.max))
                link(dve.tensor_reduce(gm[:, :], go[:, :, :], AX.X, ALU.max))
                link(dve.tensor_tensor(go[:, :, :], go[:, :, :], bc(gm), ALU.subtract))
                dve.wait_ge(g_sems["fin_act"], 1)
                link(dve.tensor_reduce(gs[:, :], ge[:, :, :], AX.X, ALU.add))
                dve.wait_ge(g_sems["fin_act"], 2)
                link(dve.tensor_tensor(go[:, :, :], go[:, :, :], bc(gw), ALU.subtract))
                link(dve.tensor_tensor(go[:, :, :], go[:, :, :], x_nat[:, :, :], ALU.add))
                link(dve.tensor_reduce(gm[:, :], go[:, :, :], AX.X, ALU.add))
                link(dve.tensor_scalar(gm[:, :], gm[:, :], 1.0 / C, None, ALU.mult))
                link(dve.tensor_tensor(go[:, :, :], go[:, :, :], bc(gm), ALU.subtract))
                dve.wait_ge(g_sems["fin_act"], 3)
                link(dve.tensor_reduce(gs[:, :], ge[:, :, :], AX.X, ALU.add))
                dve.wait_ge(g_sems["fin_act"], 4)
                link(dve.reciprocal(gm[:, :], gw[:, :]))
                link(dve.tensor_tensor(ge[:, :, :], go[:, :, :], bc(gm), ALU.mult))

        @block.scalar
        def _(act):
            act.preload_act_table_set("natural_log_exp_and_others")
            act.wait_ge(xnat_in, 16)
            act.activation(x3[:, :, 0:C], x_nat[:, :, :], ACT.Copy).then_inc(xs_ready, 1)

            def copy_keys(key, bank, g0, n):
                src = bank.rearrange("p (g k) -> p g k", g=n)
                act.activation(key[:, g0:g0 + n, 0:9], src[:, :, 0:9], ACT.Copy)
                return act.activation(key[:, g0:g0 + n, 10:26], src[:, :, 9:25], ACT.Copy)

            act.wait_ge(keyt_done, 1)
            copy_keys(keyl, acc[:, 0:Q], 0, 5)
            copy_keys(keyr, acc[:, Q:2 * Q], 0, 5).then_inc(keys_ready, 1)
            act.wait_ge(xs_rest, 1)
            act.activation(x3[:, :, XC:XC + C], x_rest, ACT.Copy).then_inc(xs_ready, 1)

            def evacuate(g, s):
                if g == sums_group and s == 0:
                    for j in range(J):
                        act.wait_ge(se_out[j], 16)
                act.wait_ge(built[s], g + 1)
                if s == 3:
                    w0 = SINGLE * WD
                    act.activation(adj4[0:Q, g, :, w0:w0 + WD],
                                   dense[0:Q, 0:G * WD].rearrange("p (h e) -> p h e", h=G), ACT.Copy)\
                       .then_inc(evac[3], 1)
                else:
                    w0 = SETS[s][0] * WD
                    act.activation(adj4[0:Q, g, :, w0:w0 + 8 * WD].rearrange("p h (b e) -> p b h e", b=2),
                                   pset[s][0:Q, :, 0:4 * WD * G].rearrange("p b (h e) -> p b h e", h=G), ACT.Copy)\
                       .then_inc(evac[s], 1)

            for g in range(-1, G + 1):
                h = g - 1
                b = g + 1 < G
                if b:
                    evacuate(g + 1, 0)
                    evacuate(g + 1, 3)
                if h >= 0:
                    act.wait_ge(t_ready, h + 1)
                    act.activation(ut[:, :], dense[:, 0:Q], ACT.Copy)
                    act.activation(vt[:, :], dense[0:KB, Q:2 * Q], ACT.Copy).then_inc(ut_ready, 1)
                if b:
                    evacuate(g + 1, 1)
                if h >= 0:
                    act.wait_ge(h_ready, h + 1)
                    act.activation(ht[:, :], dense[:, 256:256 + Q], ACT.Relu).then_inc(ht_ready, 1)
                if b:
                    evacuate(g + 1, 2)
                if h >= 0:
                    act.wait_ge(zp_ready, h + 1)
                    if h >= 1:
                        act.wait_ge(base_ready, h)
                    act.activation(zs[:, :], dense[0:Q, 0:3 * C], ACT.Copy).then_inc(zs_ready, 1)
                if g == 0:
                    for i, key in enumerate((keyl, keyr)):
                        act.wait_ge(keyt_done, 2 + i)
                        copy_keys(key, dense[:, 0:4 * Q], 5, G - 5).then_inc(keys_ready, 1)
            na = 0
            for i, (a, b) in enumerate(BATCHES):
                n = b - a
                act.wait_ge(fch, at["shifted", i])
                act.activation(f_e[:, 0:n, :], f_o[:, 0:n, :], ACT.Exp).then_inc(fact, 1)
                act.wait_ge(fch, at["sums", i])
                act.activation(f_l[:, 0:n], f_s[:, 0:n], ACT.Ln).then_inc(fact, 1)
                act.wait_ge(fch, at["variance", i])
                act.activation(f_g[:, 0:n], f_mv[:, 0:n, 1], ACT.Ln, bias=EPS).then_inc(fact, 1)
                act.wait_ge(fact, na + 3)
                act.activation(f_y[:, 0:n], f_g[:, 0:n], ACT.Exp, scale=-0.5).then_inc(fact, 1)
                na += 4

            act.wait_ge(flag_ready, 1)
            act.wait_ge(o_out[0], 16 * ((len(BATCHES) + 1) // 2))
            act.wait_ge(o_out[1], 16 * (len(BATCHES) // 2))
            missed = act.value_load(flag[0:1, 0:1], min_val=0, max_val=1)
            with act.If(missed):
                with act.Fori(0, G) as g:
                    act.wait_ge(g_sems["t_ready"], g + 1)
                    act.activation(ut[:, :], dense[:, 0:Q], ACT.Copy)
                    act.activation(g_vt, dense[0:2, Q:2 * Q], ACT.Copy).then_inc(g_sems["ut_ready"], 1)
                    act.wait_ge(g_sems["h_ready"], g + 1)
                    act.activation(ht[:, :], dense[:, 256:256 + Q], ACT.Relu).then_inc(g_sems["ht_ready"], 1)
                    act.wait_ge(g_sems["zp_ready"], g + 1)
                    act.wait_ge(g_sems["base_ready"], g + 1)
                    act.wait_ge(g_sems["z_stored"], 16 * (g + 1))
                    act.activation(zs[:, :], dense[0:Q, 0:3 * C], ACT.Copy).then_inc(g_sems["zs_ready"], 1)
                act.wait_ge(g_sems["fin"], 4)
                act.activation(ge[:, :, :], go[:, :, :], ACT.Exp).then_inc(g_sems["fin_act"], 1)
                act.wait_ge(g_sems["fin"], 5)
                act.activation(gw[:, :], gs[:, :], ACT.Ln).then_inc(g_sems["fin_act"], 1)
                act.wait_ge(g_sems["fin"], 10)
                act.activation(ge[:, :, :], go[:, :, :], ACT.Square).then_inc(g_sems["fin_act"], 1)
                act.wait_ge(g_sems["fin"], 11)
                act.activation(gw[:, :], gs[:, :], ACT.Sqrt, scale=1.0 / C, bias=EPS).then_inc(g_sems["fin_act"], 1)

        @block.tensor
        def _(pe):
            pe.wait_ge(consts, 3)
            pe.wait_ge(sampb_ready, 1)
            pe.matmul(acc[0:Q, 0:Q], samp_b, ident[0:Q, 0:Q], start=True, stop=True).then_inc(sampm_ready, 1)
            pe.wait_ge(rowidx_ready, 1)
            pe.wait_ge(key_ready, 1)
            pe.transpose(acc[:, 0:Q], lo_f[:, 0, :], ident[0:Q, 0:Q])
            pe.transpose(acc[:, Q:2 * Q], key_f[:, 0, :], ident[0:Q, 0:Q]).then_inc(keyt_done, 1)

            def build(g, s):
                if g >= 1:
                    pe.wait_ge(evac[s], g)
                pe.wait_ge(oh_ready[s], g + 1)
                for i in range(8):
                    ins = pe.matmul(
                        pset[s][0:Q, i // 4, 0:4 * WD * G].rearrange("p (h e) -> p h e", h=G)[:, :, i % 4 * WD:(i % 4 + 1) * WD],
                        ohl[s][:, i // 2, :, i % 2], ohr[s][:, i // 2, :, i % 2], start=True, stop=True)
                ins.then_inc(built[s], 1)

            def build_single(g):
                pe.wait_ge(oh_ready[0], g + 1)
                if g >= 3:
                    pe.wait_ge(zs_ready, g - 2)
                elif g >= 1:
                    pe.wait_ge(evac[3], g)
                    pe.wait_ge(keys_ready, 3 if g == 2 else 1)
                pe.matmul(dense[0:Q, 0:G * WD], ohl[0][:, 4, :, 0], ohr[0][:, 4, :, 0], start=True, stop=True)\
                  .then_inc(built[3], 1)

            def layer1(g, h0, h1):
                if h0 == 0:
                    pe.wait_ge(evac[2], g + 1)
                    if g == 0:
                        pe.wait_ge(keys_ready, 1)
                    if g >= 1:
                        pe.wait_ge(acc_read, g)
                for h in range(h0, h1):
                    ins = pe.matmul(acc[0:Q, 0:XW], adj4[0:Q, g, h, :], x3[:, h, :],
                                    start=(h == 0), stop=(h == G - 1))
                if h1 == G:
                    ins.then_inc(acc_done, 1)

            def layer2(g, h0, h1):
                for h in range(h0, h1):
                    ins = pe.matmul(bank2(g)[0:Q, :], adj4[0:Q, g, h, :], z3[:, h, :],
                                    start=(h == 0), stop=(h == G - 1))
                if h1 == G:
                    ins.then_inc(acc2_done, 1)

            for g in range(-1, G + 1):
                h = g - 1
                b, l, d = g + 1 < G, 0 <= g < G, h >= 0
                if b:
                    build(g + 1, 0)
                if g == 0:
                    pe.wait_ge(xs_ready, 3)
                if g == G - 1:
                    pe.wait_ge(evac[0], G)
                    pe.wait_ge(z3_ready, 8)
                    layer2(0, 0, 8)
                if l:
                    layer1(g, 0, 8)
                if b:
                    build_single(g + 1)
                if b:
                    build(g + 1, 1)
                if l:
                    layer1(g, 8, 11)
                if g == G:
                    pe.wait_ge(z3_ready, 16)
                    layer2(0, 8, 16)
                if d:
                    pe.wait_ge(u_ready, h + 1)
                    if h % 5 == 0:
                        pe.wait_ge(se_parts, h // 5 + 1)
                    if h + 2 < G:
                        pe.wait_ge(evac[3], h + 3)
                    else:
                        pe.wait_ge(zs_ready, h)
                    pe.transpose(dense[:, 0:Q], u[:, :], ident[0:Q, 0:Q])
                    pe.matmul(dense[0:KB, Q:2 * Q], stats[:, h, :], ident16[0:Q, :], start=True, stop=True)\
                      .then_inc(t_ready, 1)
                if l:
                    layer1(g, 11, 17)
                if b:
                    build(g + 1, 2)
                if g == G:
                    pe.wait_ge(z3_ready, G - 2)
                    layer2(0, 16, G - 2)
                if d:
                    if h == 0:
                        pe.wait_ge(w_in, 16 * 4)
                        pe.wait_ge(bw_ready, 1)
                    pe.wait_ge(ut_ready, h + 1)
                    pe.matmul(dense[:, 256:256 + Q], w1c[:, :], ut[:, :], start=True, stop=False)
                    pe.matmul(dense[:, 256:256 + Q], bw[:, 0:HID], vt[:, :], start=False, stop=True).then_inc(h_ready, 1)
                if l:
                    layer1(g, 17, G)
                if g == G:
                    layer2(1, 0, 8)
                if g == 0:
                    pe.wait_ge(key_ready, 2)
                    pe.wait_ge(evac[3], 2)
                    for i, key in enumerate((lo_f, key_f)):
                        if i == 1:
                            pe.wait_ge(keys_ready, 2)
                        for j in range(1, J):
                            ins = pe.transpose(dense[:, (j - 1) * Q:j * Q], key[:, j, :], ident[0:Q, 0:Q])
                        ins.then_inc(keyt_done, 1)
                if d:
                    pe.wait_ge(ht_ready, h + 1)
                    pe.matmul(dense[0:Q, 0:2 * C], ht[:, :], w2c[:, :], start=True, stop=True)
                    pe.matmul(dense[0:Q, 2 * C:3 * C], vt[:, :], bw[:, HID:HID + C], start=True, stop=True).then_inc(zp_ready, 1)

            layer2(1, 8, G - 2)
            layer2(2, 0, G - 2)
            pe.wait_ge(z3_ready, G)
            for g in range(3):
                layer2(g, G - 2, G)
            for g in range(3, G):
                if g >= 6:
                    pe.wait_ge(acc2_read, g - 5)
                layer2(g, 0, G)
                if g == BATCHES[0][1]:
                    pe.wait_ge(deg_ready, 1)
                    pe.wait_ge(zs_ready, G)
                    pe.matmul(dense[0:1, 0:1], deg_sum[:, :], ones_f[:, :], start=True, stop=True).then_inc(degs_ready, 1)

            pe.wait_ge(flag_ready, 1)
            pe.wait_ge(o_out[0], 16 * ((len(BATCHES) + 1) // 2))
            pe.wait_ge(o_out[1], 16 * (len(BATCHES) // 2))
            missed = pe.value_load(flag[0:1, 0:1], min_val=0, max_val=1)
            with pe.If(missed):
                pe.wait_ge(g_sems["consts"], 3)
                pe.wait_ge(g_sems["loaded"], 16 * 6)
                for layer in range(2):
                    if layer:
                        pe.wait_ge(g_sems["sum_ready"], 1)
                    for b in range(NBANK):
                        ins = pe.matmul(g_acc[b][:, :], g_zero[:, 0:128], g_zero[:, :], start=True, stop=False)
                    ins.then_inc(g_sems[f"chunk_done{layer}"], 1)
                    with pe.Fori(0, EC) as c:
                        pe.wait_ge(g_sems[f"gathered{layer}"], 16 * (c + 1))
                        pe.wait_ge(g_sems[f"attr_ready{layer}"], c + 1)
                        pe.wait_ge(g_sems[f"oh_ready{layer}"], c + 1)
                        for g in range(G):
                            b, n = divmod(g, BANK_GROUPS)
                            ins = pe.matmul(g_acc[b][0:Q, n * MW:(n + 1) * MW], g_onehot[:, g * Q:(g + 1) * Q],
                                            g_msg[:, :], start=False, stop=False)
                        ins.then_inc(g_sems[f"chunk_done{layer}"], 1)
                    for b in range(NBANK):
                        ins = pe.matmul(g_acc[b][:, :], g_zero[:, 0:128], g_zero[:, :], start=False, stop=True)
                    ins.then_inc(g_sems["acc_done"], 1)
                    if layer == 0:
                        with pe.Fori(0, G) as g:
                            pe.wait_ge(g_sems["u_ready"], 2 * g + 2)
                            pe.transpose(dense[:, 0:Q], u[:, :], ident[0:Q, 0:Q])
                            pe.transpose(dense[0:2, Q:2 * Q], g_v[:, :], ident[0:Q, 0:Q]).then_inc(g_sems["t_ready"], 1)
                            pe.wait_ge(g_sems["ut_ready"], g + 1)
                            pe.matmul(dense[:, 256:256 + Q], w1c[:, :], ut[:, :], start=True, stop=False)
                            pe.matmul(dense[:, 256:256 + Q], g_bw1, g_vt, start=False, stop=True).then_inc(g_sems["h_ready"], 1)
                            pe.wait_ge(g_sems["ht_ready"], g + 1)
                            pe.matmul(dense[0:Q, 0:2 * C], ht[:, :], w2c[:, :], start=True, stop=True)
                            pe.matmul(dense[0:Q, 2 * C:3 * C], g_vt, g_bw2, start=True, stop=True).then_inc(g_sems["zp_ready"], 1)

        @block.sync
        def _(sp):
            with nc.allow_non_contiguous_dma(reason="one target per partition"):
                sp.dma_start(samp, dst[:, 0:1]).then_inc(samp_in, 16)
            sp.dma_start(x_nat[:, :, :], x.rearrange("(g q) c -> q g c", q=Q)).then_inc(xnat_in, 16)
            sp.dma_start(w1c[0:C, :], W1[C:2 * C, :]).then_inc(w_in, 16)
            sp.dma_start(w1c[C:2 * C, :], W1[0:C, :]).then_inc(w_in, 16)
            sp.dma_start(w2c[:, 0:C], W2[HID:2 * HID, :]).then_inc(w_in, 16)
            sp.dma_start(w2c[:, C:2 * C], W2[0:HID, :]).then_inc(w_in, 16)
            for col, n, b, w in ((0, HID, b1, W1[2 * C:2 * C + 1, :]), (HID, C, b2, W2[2 * HID:2 * HID + 1, :])):
                sp.dma_start(brows[0:3, col:col + n], b.rearrange("(a n) -> a n", a=1).broadcast_to([3, n])).then_inc(b_in, 16)
                sp.dma_start(brows[3:KB, col:col + n], w.broadcast_to([KB - 3, n])).then_inc(b_in, 16)
            with nc.allow_non_contiguous_dma(reason="one number per node"):
                for j in range(J):
                    sp.wait_ge(se_ready, (j + 1) * WD)
                    sp.dma_start(se_dram[j * Q * WD:(j + 1) * Q * WD].rearrange("(p r) -> p r", r=WD), se_w[:, j, :])\
                      .then_inc(se_out[j], 16)
                    sp.wait_ge(se_out[j], 16)
                    sp.dma_start(se[:, 5 * j:5 * j + 5],
                                 se_dram[j * Q * WD:(j + 1) * Q * WD].rearrange("(g q) -> q g", q=Q))\
                      .then_inc(se_in[j], 16)
            for i, (a, b) in enumerate(BATCHES):
                sp.wait_ge(fch, at["stored", i])
                sp.dma_start(out[a * Q:b * Q, :].rearrange("(g q) c -> q g c", q=Q),
                             f_v[i % 2][:, 0:b - a, :]).then_inc(o_out[i % 2], 16)

            sp.wait_ge(flag_ready, 1)
            sp.wait_ge(o_out[0], 16 * ((len(BATCHES) + 1) // 2))
            sp.wait_ge(o_out[1], 16 * (len(BATCHES) // 2))
            missed = sp.value_load(flag[0:1, 0:1], min_val=0, max_val=1)
            with sp.If(missed):
                sp.dma_start(g_edges[:, :, :], edges[0:E, :].rearrange("(p j) t -> p j t", p=Q)).then_inc(g_sems["loaded"], 16)
                sp.dma_start(g_attr[:, :], edge_attr[0:E, 0].rearrange("(p j) -> p j", p=Q)).then_inc(g_sems["loaded"], 16)
                for t, b, w in ((g_bw1, b1, W1[2 * C:2 * C + 1, :]), (g_bw2, b2, W2[2 * HID:2 * HID + 1, :])):
                    sp.dma_start(t[0:1, :], b.rearrange("(a n) -> a n", a=1)).then_inc(g_sems["loaded"], 16)
                    sp.dma_start(t[1:2, :], w).then_inc(g_sems["loaded"], 16)
                with sp.Fori(0, G) as g:
                    sp.wait_ge(g_sems["zs_ready"], g + 1)
                    sp.dma_start(gz_dram[bass.ds(g * Q, Q), :], zs[:, 0:C]).then_inc(g_sems["z_stored"], 16)
                sp.wait_ge(g_sems["fin"], 13)
                sp.dma_start(out.rearrange("(g q) c -> q g c", q=Q), ge[:, :, :]).then_inc(g_sems["out_stored"], 16)
                sp.wait_ge(g_sems["out_stored"], 16)


def kernel(x, src, dst, edge_weight1, L0_gnn_W1, L0_gnn_b1, L0_gnn_W2, L0_gnn_b2):
    import numpy as _np
    import concourse.bacc as _bacc
    from concourse import mybir as _mybir
    from concourse.bass_utils import run_bass_kernel_spmd as _run

    nc = _bacc.Bacc("TRN2", target_bir_lowering=False, num_devices=1)
    E = src.shape[0]
    arrays, args = {}, []
    edges = _np.stack([_np.asarray(src), _np.asarray(dst)], axis=1)
    edges = _np.concatenate([edges, _np.full((128, 2), N, edges.dtype)], axis=0)
    dst_rows = _np.asarray(dst).reshape(Q, -1)
    attr = _np.concatenate([_np.asarray(edge_weight1)[:, 0], _np.zeros(128, _np.float32)])[:, None]
    for name, a in (("x", x), ("dst", dst_rows), ("edges", edges), ("edge_attr", attr), ("W1", L0_gnn_W1), ("b1", L0_gnn_b1),
                    ("W2", L0_gnn_W2), ("b2", L0_gnn_b2)):
        a = _np.ascontiguousarray(a)
        arrays[f"in_{name}"] = a
        args.append(nc.dram_tensor(f"in_{name}", a.shape, _mybir.dt.from_np(a.dtype), kind="ExternalInput").ap())
    out = nc.dram_tensor("out_0", [N, C], _mybir.dt.float32, kind="ExternalOutput").ap()
    gnn(nc, *args, out, E)
    r = _run(nc, [arrays], core_ids=[0])
    return r.results[0]["out_0"]
```
